# Optimizing a Trainium2 kernel written in Bass

```python
import numpy as np
import jax
import jax.numpy as jnp

def _softmax(x, axis=-1):
    return jax.nn.softmax(x, axis=axis)

def _gelu(x):
    return jax.nn.gelu(x, approximate=True)

def _silu(x):
    return jax.nn.silu(x)

def _sigmoid(x):
    return jax.nn.sigmoid(x)

def _layernorm(x, axis=-1, eps=1e-05):
    m = jnp.mean(x, axis=axis, keepdims=True)
    v = jnp.var(x, axis=axis, keepdims=True)
    return (x - m) / jnp.sqrt(v + eps)

def _scatter_add(tgt, idx, src, axis=0):
    return tgt.at[idx].add(src)

def _segment_sum(src, seg, n):
    return jax.ops.segment_sum(src, seg, n)
kernel_name = 'mk_xattn_ffn_d1_seqx_r8_c5433c'

def setup_inputs(seed: int=0):
    np.random.seed(seed)
    _w = jnp.asarray

    def _rec_inputs():
        import jax
        import jax.numpy as jnp
        _rk = jax.random.key(seed)
        x = 7.22e-05 + 1 * jax.random.normal(jax.random.fold_in(_rk, 1), (16, 128, 128), jnp.float32)
        _lenS = 128 - jax.random.randint(jax.random.fold_in(_rk, 7), (16,), 0, max(1, 128 // 4) + 1, jnp.int32)
        _lenS2 = 128 - jax.random.randint(jax.random.fold_in(_rk, 8), (16,), 0, max(1, 128 // 4) + 1, jnp.int32)
        _ctx_1024P = jax.random.normal(jax.random.fold_in(_rk, 11), (16, 16, 128), jnp.float32)
        _ctx_1024c = jax.random.dirichlet(jax.random.fold_in(_rk, 511), 0.3 * jnp.ones((16,), jnp.float32), (16, 128))
        _ctx_1024t = jnp.einsum('bsk,bkd->bsd', _ctx_1024c, _ctx_1024P)
        _ctx_1024t = _ctx_1024t * jax.lax.rsqrt(jnp.mean(jnp.square(_ctx_1024t)) + 1e-12) * 0.953939
        ctx_1024 = 4.13588e-05 + 0.999923 * (_ctx_1024t + 0.3 * jax.random.normal(jax.random.fold_in(_rk, 611), (16, 128, 128), jnp.float32))
        return (x, ctx_1024)
    x, ctx_1024 = _rec_inputs()

    def _L0_xattn_setup():
        import jax, jax.numpy as jnp
        import numpy as np
        D_MODEL = 128
        NHEAD = 16
        HEAD_DIM = D_MODEL // NHEAD
        key = jax.random.key(seed)
        ks = jax.random.split(key, 11)
        B, S, D = (4, 256, D_MODEL)
        scale = 1.0 / np.sqrt(D)
        inp = {'q': jax.random.normal(ks[0], (B, S, D), jnp.float32), 'k': jax.random.normal(ks[1], (B, S, D), jnp.float32), 'v': jax.random.normal(ks[2], (B, S, D), jnp.float32), 'Wq': jax.random.normal(ks[3], (D, D), jnp.float32) * scale, 'bq': jnp.zeros((D,), jnp.float32), 'Wk': jax.random.normal(ks[4], (D, D), jnp.float32) * scale, 'bk': jnp.zeros((D,), jnp.float32), 'Wv': jax.random.normal(ks[5], (D, D), jnp.float32) * scale, 'bv': jnp.zeros((D,), jnp.float32), 'Wo': jax.random.normal(ks[6], (D, D), jnp.float32) * scale, 'bo': jnp.zeros((D,), jnp.float32)}
        return inp
    _L0_xattn_all = _L0_xattn_setup()
    _L0_xattn_in = {k: v for k, v in _L0_xattn_all.items() if k in ('Wq', 'bq', 'Wk', 'bk', 'Wv', 'bv', 'Wo', 'bo')}
    del _L0_xattn_all

    def _L0_ffn_setup():
        import jax, jax.numpy as jnp
        import numpy as np
        DIM = 128
        HIDDEN = 512
        E = 8
        B, S = (2, 512)
        key = jax.random.key(seed)
        ks = jax.random.split(key, 8)
        sd = 1.0 / np.sqrt(DIM)
        sh = 1.0 / np.sqrt(HIDDEN)
        return {'x': jax.random.normal(ks[0], (B, S, DIM), dtype=jnp.float32), 'router_w': jax.random.uniform(ks[1], (DIM, E), jnp.float32, -sd, sd), 'router_b': jax.random.uniform(ks[2], (E,), jnp.float32, -sd, sd), 'w1': jax.random.uniform(ks[3], (E, DIM, 2 * HIDDEN), jnp.float32, -sd, sd), 'b1': jax.random.uniform(ks[4], (E, 2 * HIDDEN), jnp.float32, -sd, sd), 'w2': jax.random.uniform(ks[5], (E, HIDDEN, DIM), jnp.float32, -sh, sh), 'b2': jax.random.uniform(ks[6], (E, DIM), jnp.float32, -sh, sh)}
    _L0_ffn_all = _L0_ffn_setup()
    _L0_ffn_in = {k: v for k, v in _L0_ffn_all.items() if k in ('router_w', 'router_b', 'w1', 'b1', 'w2', 'b2')}
    del _L0_ffn_all
    return {'x': x, 'ctx_1024': ctx_1024, 'L0_xattn_Wq': _L0_xattn_in['Wq'], 'L0_xattn_bq': _L0_xattn_in['bq'], 'L0_xattn_Wk': _L0_xattn_in['Wk'], 'L0_xattn_bk': _L0_xattn_in['bk'], 'L0_xattn_Wv': _L0_xattn_in['Wv'], 'L0_xattn_bv': _L0_xattn_in['bv'], 'L0_xattn_Wo': _L0_xattn_in['Wo'], 'L0_xattn_bo': _L0_xattn_in['bo'], 'L0_ffn_router_w': _L0_ffn_in['router_w'], 'L0_ffn_router_b': _L0_ffn_in['router_b'], 'L0_ffn_w1': _L0_ffn_in['w1'], 'L0_ffn_b1': _L0_ffn_in['b1'], 'L0_ffn_w2': _L0_ffn_in['w2'], 'L0_ffn_b2': _L0_ffn_in['b2']}

def reference(x, ctx_1024, L0_xattn_Wq, L0_xattn_bq, L0_xattn_Wk, L0_xattn_bk, L0_xattn_Wv, L0_xattn_bv, L0_xattn_Wo, L0_xattn_bo, L0_ffn_router_w, L0_ffn_router_b, L0_ffn_w1, L0_ffn_b1, L0_ffn_w2, L0_ffn_b2):
    import jax
    import jax.numpy as jnp

    def _L0_xattn_ref(q, k, v, Wq, bq, Wk, bk, Wv, bv, Wo, bo):
        import jax, jax.numpy as jnp
        import numpy as np
        D_MODEL = 128
        NHEAD = 16
        HEAD_DIM = D_MODEL // NHEAD
        B, S, D = q.shape
        H, Hd = (NHEAD, HEAD_DIM)
        qh = (q @ Wq.T + bq).reshape(B, S, H, Hd).transpose(0, 2, 1, 3)
        kh = (k @ Wk.T + bk).reshape(B, S, H, Hd).transpose(0, 2, 1, 3)
        vh = (v @ Wv.T + bv).reshape(B, S, H, Hd).transpose(0, 2, 1, 3)
        scores = jnp.einsum('bhqd,bhkd->bhqk', qh, kh) / jnp.sqrt(jnp.float32(Hd))
        attn = jax.nn.softmax(scores, axis=-1)
        out = jnp.einsum('bhqk,bhkd->bhqd', attn, vh)
        out = out.transpose(0, 2, 1, 3).reshape(B, S, D)
        return out @ Wo.T + bo

    def _L0_ffn_ref(x, router_w, router_b, w1, b1, w2, b2):
        import jax, jax.numpy as jnp
        import numpy as np
        DIM = 128
        HIDDEN = 512
        E = 8
        B, S = (2, 512)
        logits = jnp.einsum('bsd,de->bse', x, router_w) + router_b
        probs = jax.nn.softmax(logits, axis=-1)
        top1 = jnp.argmax(probs, axis=-1)
        out = jnp.zeros_like(x)
        for i in range(E):
            h = jnp.einsum('bsd,df->bsf', x, w1[i]) + b1[i]
            a, g = jnp.split(h, 2, axis=-1)
            y = jnp.einsum('bsh,hd->bsd', a * jax.nn.sigmoid(g), w2[i]) + b2[i]
            out = out + jnp.where((top1 == i)[..., None], y, 0.0)
        return out
    x = x + _L0_xattn_ref(_layernorm(x, axis=-1), ctx_1024, ctx_1024, L0_xattn_Wq, L0_xattn_bq, L0_xattn_Wk, L0_xattn_bk, L0_xattn_Wv, L0_xattn_bv, L0_xattn_Wo, L0_xattn_bo)
    x = x + _L0_ffn_ref(_layernorm(x, axis=-1), L0_ffn_router_w, L0_ffn_router_b, L0_ffn_w1, L0_ffn_b1, L0_ffn_w2, L0_ffn_b2)
    return x

_drawn_inputs = setup_inputs


def setup_inputs(seed=0):
    import zlib

    import numpy as np

    out = dict(_drawn_inputs(seed))
    spreads = {'L0_xattn_bq': (0.0, 0.1),
     'L0_xattn_bk': (0.0, 0.8),
     'L0_xattn_bv': (0.0, 0.1),
     'L0_xattn_bo': (0.0, 0.1)}
    factors = {'L0_ffn_b1': 4.268}
    for name, (base, spread) in spreads.items():
        noise = np.random.default_rng([zlib.crc32(name.encode()), seed]).standard_normal(out[name].shape)
        drawn = base * np.exp(spread * noise) if base else spread * noise
        out[name] = jnp.asarray(drawn.astype(out[name].dtype))
    for name, factor in factors.items():
        out[name] = (out[name] * factor).astype(out[name].dtype)
    return out
```

```python
import concourse.bass as bass
from concourse import mybir
from contextlib import ExitStack

B = 16
S = 128
D = 128
HEADS = 16
HD = D // HEADS
E = 8
F = 512
PAIRS = B // 2
TOKENS = B * S
PAGES = TOKENS // S
TILES = PAGES + E - 1
PARTS = 3
SLOTS = 6
ROWS = SLOTS * HD
HALF = HEADS // 2
EPS = 1e-5


def xattn_ffn(nc, x, ctx_in, wq, wk, wv, wo, bq, bk, bv, bo, rw, rb, w1, b1, w2, b2, out):
    f32, bf16, f16 = mybir.dt.float32, mybir.dt.bfloat16, mybir.dt.float16
    i32, u32 = mybir.dt.int32, mybir.dt.uint32
    ALU = mybir.AluOpType
    ACT = mybir.ActivationFunctionType
    X = mybir.AxisListType.X

    qk_dram = nc.dram_tensor("qk_stacked", (B, 2, ROWS, 2, HALF * S), bf16).ap()
    rows_dram = nc.dram_tensor("token_rows", (TOKENS, 2 * D), f32).ap()

    with ExitStack() as stack:
        def sb(name, shape, dt=f32):
            return stack.enter_context(nc.sbuf_tensor(name, shape, dt))

        def sem(name):
            return stack.enter_context(nc.semaphore(name))

        ident = sb("ident", [128, 128])
        ident_bf = sb("ident_bf", [128, 128], bf16)
        below = sb("below", [128, 128], bf16)
        ones_bf = sb("ones_bf", [128, 128], bf16)
        ones = sb("ones", [128, 128])
        pick = sb("pick", [128, HALF, S], bf16)
        count = sb("count", [128, 128])
        expert_of = sb("expert_of", [128, 1])
        token_no = sb("token_no", [128, 2])
        eps = sb("eps", [128, 1])
        power = sb("power", [128, B])

        wq_sb, wk_sb, wv_sb, wo_sb = (sb(n, [128, 128]) for n in ("wq_sb", "wk_sb", "wv_sb", "wo_sb"))
        bq_sb, bk_sb, bv_sb = (sb(n, [128, 1]) for n in ("bq_sb", "bk_sb", "bv_sb"))
        bo_sb = sb("bo_sb", [128, D])
        rw_sb = sb("rw_sb", [128, E])
        rb_sb = sb("rb_sb", [128, E])
        w1_sb = sb("w1_sb", [128, E * 2 * F])
        b1_sb = sb("b1_sb", [128, E * 2 * F])
        w2_sb = sb("w2_sb", [128, E * F])
        b2_sb = sb("b2_sb", [128, E * D])

        x_all = sb("x_all", [128, B, D])
        ctx_all = sb("ctx_all", [128, B, D])
        v_all = sb("v_all", [128, B, D])
        xb_all = x_all
        bv_cols = sb("bv_cols", [128, 128])
        obias = sb("obias", [128, D])
        stats1 = sb("stats1", [128, B, 6])
        mv1 = sb("mv1", [128, B, 2])
        var1 = sb("var1", [128, B])
        rstd1 = sb("rstd1", [128, B])
        staged = [sb(f"staged{u}", [128, 4, D]) for u in range(2)]
        stagedT = [sb(f"stagedT{u}", [128, 4 * S]) for u in range(2)]
        qkf = [sb(f"qkf{u}", [128, 2, 2 * S]) for u in range(2)]
        resid = [sb(f"resid{u}", [128, 2, 2 * S]) for u in range(2)]
        parts = [sb(f"parts{u}", [128, 2 * SLOTS, 2 * S], bf16) for u in range(2)]

        qk = [sb(f"qk{u}", [128, 2, HALF, S], bf16) for u in range(2)]
        rowmax = [sb(f"rowmax{u}", [128, HEADS]) for u in range(2)]
        maxres = [sb(f"maxres{u}", [128, HEADS]) for u in range(2)]
        maxparts = [sb(f"maxparts{u}", [128, 2, 8, HALF], bf16) for u in range(2)]
        maxT = [sb(f"maxT{u}", [128, S], bf16) for u in range(2)]
        probsT = [sb(f"probsT{f}", [128, 4 * S]) for f in range(4)]
        vpad = [sb(f"vpad{u}", [128, HEADS, 32]) for u in range(2)]
        oT = sb("oT", [128, 4 * S])
        rsum = sb("rsum", [128, HEADS])
        att = sb("att", [128, HEADS, HD])
        attT = sb("attT", [128, S])
        rows = [sb(f"rows{u}", [128, 2, D]) for u in range(2)]
        stats2 = sb("stats2", [128, 6])
        mv2 = [sb(f"mv2{u}", [128, 2]) for u in range(2)]
        var2 = [sb(f"var2{u}", [128, 1]) for u in range(2)]
        rstd2 = [sb(f"rstd2{u}", [128, 1]) for u in range(2)]
        x2T = sb("x2T", [128, S])

        logits = sb("logits", [128, 2, E])
        top = sb("top", [128, 2, 8])
        topi = sb("topi", [128, 2, 8], u32)
        onehot = sb("onehot", [128, 2, E], bf16)
        seen = sb("seen", [128, E], bf16)
        ranksel = sb("ranksel", [128, 2, E])
        rankf = sb("rankf", [128, 2])
        rank = sb("rank", [128, 2], i32)
        page = sb("page", [128, 2], i32)
        slot_i = sb("slot_i", [128, 2], i32)
        pagecode = sb("pagecode", [128, 2])
        slot = sb("slot", [128, 2])
        in_page = sb("in_page", [128, B, 128], f16)
        at_slot = sb("at_slot", [128, B, 128], f16)
        table = sb("table", [128, 128])
        occ = sb("occ", [128, 1])
        occ_bf = sb("occ_bf", [128, 1], bf16)
        tile_of = sb("tile_of", [128, 1])
        choose = sb("choose", [128, TILES])
        pad = sb("pad", [128, TILES])
        from_row = sb("from_row", [128, TILES], u32)
        to_row = sb("to_row", [128, TILES], u32)
        tile_expert = sb("tile_expert", [1, TILES], i32)

        gather_at = [sb(f"gather_at{u}", [128, 1], u32) for u in range(2)]
        scatter_at = [sb(f"scatter_at{u}", [128, 1], u32) for u in range(2)]
        got = [sb(f"got{u}", [128, 2 * D]) for u in range(2)]
        gotT = [sb(f"gotT{u}", [128, S]) for u in range(2)]
        up = [sb(f"up{u}", [128, F]) for u in range(2)]
        gate = [sb(f"gate{u}", [128, F]) for u in range(2)]
        sig = [sb(f"sig{u}", [128, F]) for u in range(2)]
        hid = [sb(f"hid{u}", [128, F]) for u in range(2)]
        hidT = [sb(f"hidT{u}", [128, F]) for u in range(2)]
        base = [sb(f"base{u}", [128, D]) for u in range(2)]
        final = [sb(f"final{u}", [128, D]) for u in range(2)]

        bank = [stack.enter_context(nc.psum_tensor(f"bank{n}", [128, 512], f32)) for n in range(8)]

        in_x, in_ctx, in_w, in_ffn = sem("in_x"), sem("in_ctx"), sem("in_w"), sem("in_ffn")
        consts = sem("consts")
        x_var, x_rstd = sem("x_var"), sem("x_rstd")
        obias_mm, bv_ready, obias_ready, xb_ready = sem("obias_mm"), sem("bv_ready"), sem("obias_ready"), sem("xb_ready")
        staged_ok, T_mm, T_ok = sem("staged_ok"), sem("T_mm"), sem("T_ok")
        P_mm, V_mm = sem("P_mm"), sem("V_mm")
        qkf_ok, high_ok, v_ok = sem("qkf_ok"), sem("high_ok"), sem("v_ok")
        resid_ok, parts_ok = sem("resid_ok"), sem("parts_ok")
        qk_out = [sem("qk_out0"), sem("qk_out1")]
        qk_in = [sem("qk_in0"), sem("qk_in1")]
        a_mm, max_ok, maxparts_ok, maxT_mm, maxT_ok = (
            sem(n) for n in ("a_mm", "max_ok", "maxparts_ok", "maxT_mm", "maxT_ok"))
        b_mm, probs_ok, vpad_ok, pv_mm, oT_ok, o_mm, att_ok, attT_mm, attT_ok, wo_mm = (
            sem(n) for n in ("b_mm", "probs_ok", "vpad_ok", "pv_mm", "oT_ok", "o_mm", "att_ok",
                             "attT_mm", "attT_ok", "wo_mm"))
        x2_var, x2_rstd, x2n_ok, x2T_mm, x2T_ok, lg_mm, lg_read = (
            sem(n) for n in ("x2_var", "x2_rstd", "x2n_ok", "x2T_mm", "x2T_ok", "lg_mm", "lg_read"))
        onehot_ok, rank_mm, rank_read, routed = (
            sem(n) for n in ("onehot_ok", "rank_mm", "rank_read", "routed"))
        rows_out = [sem("rows_out0"), sem("rows_out1")]
        table_mm, occ_ok, tileno_mm, choose_ok, index_mm, index_ok = (
            sem(n) for n in ("table_mm", "occ_ok", "tileno_mm", "choose_ok", "index_mm", "index_ok"))
        gathered = [sem("gathered0"), sem("gathered1")]
        scattered = [sem("scattered0"), sem("scattered1")]
        gotT_mm, gotT_ok, h_mm, gate_ok, up_ok, sig_ok, hid_ok, hidT_mm, hidT_ok, y_mm, base_ok, final_ok = (
            sem(n) for n in ("gotT_mm", "gotT_ok", "h_mm", "gate_ok", "up_ok", "sig_ok", "hid_ok",
                             "hidT_mm", "hidT_ok", "y_mm", "base_ok", "final_ok"))

        N_IN_W = 12
        N_IN_FFN = 4

        def wait(eng, s, value):
            if isinstance(value, int) and value <= 0:
                return
            eng.wait_ge(s, value)

        def run_front(ahead, step):
            def both(eng):
                ahead(0, 0)
                for u in range(2):
                    ahead(u + 1, 1 - u)
                    step(u, u, 0)
                with eng.Fori(1, PAIRS // 2 - 1) as i:
                    for u in range(2):
                        ahead(2 * i + u + 1, 1 - u)
                        step(2 * i + u, u, i)
                ahead(PAIRS - 1, 1)
                step(PAIRS - 2, 0, PAIRS // 2 - 1)
                step(PAIRS - 1, 1, PAIRS // 2 - 1)
            return both

        def run_slots(eng, slot_fn):
            def peeled(b):
                slot_fn(b, b // 2, b % 2, 0 <= b < B, b + 1 < B, 1 <= b <= B, 2 <= b <= B + 1)
            for b in range(-1, 4):
                peeled(b)
            with eng.Fori(2, PAIRS - 1) as p:
                for u in range(2):
                    slot_fn(2 * p + u, p, u, True, True, True, True)
            for b in range(B - 2, B + 2):
                peeled(b)

        def run_tiles(eng, step_fn):
            def peeled(j):
                step_fn(j, j // 2, j % 2, lambda k: 0 <= j + k < TILES)
            for j in range(4):
                peeled(j)
            with eng.Fori(2, (TILES - 3) // 2) as i:
                for u in range(2):
                    step_fn(2 * i + u, i, u, lambda k: True)
            for j in range(2 * ((TILES - 3) // 2), TILES + 2):
                peeled(j)

        block = stack.enter_context(nc.Block())

        @block.sync
        def _(sp):
            sp.dma_start(x_all[:, :, :], x.rearrange("b t d -> t b d")).then_inc(in_x, 16)
            sp.dma_start(ctx_all[:, :, :], ctx_in.rearrange("b t d -> t b d")).then_inc(in_ctx, 16)
            for dst, src in ((wq_sb, wq), (wk_sb, wk), (wv_sb, wv), (wo_sb, wo), (rw_sb, rw),
                             (bq_sb, bq), (bk_sb, bk), (bv_sb, bv)):
                sp.dma_start(dst[:, :], src).then_inc(in_w, 16)
            sp.dma_start(bo_sb[:, :], bo.partition_broadcast(128)).then_inc(in_w, 16)
            sp.dma_start(rb_sb[:, :], rb.partition_broadcast(128)).then_inc(in_w, 16)

            with sp.Fori(0, PAIRS // 2) as i:
                for u in range(2):
                    pair = 2 * i + u
                    sp.wait_ge(parts_ok, 2 * pair + 2)
                    for v in range(2):
                        dst = qk_dram[bass.ds(2 * pair + v, 1), :, :, :, :].rearrange(
                            "o q (r d) p (i t) -> (d p i) (o q r) t", r=SLOTS, t=S)
                        sp.dma_start(dst, parts[u][:, :, v * S:(v + 1) * S]).then_inc(qk_out[u], 16)

            def load_qk(b, u):
                for p in range(2):
                    src = qk_dram[bass.ds(b, 1), :, :, p, :].rearrange("o q k f -> k (o q) f")
                    dst = qk[u][64 * p:64 * p + ROWS, :, :, :].rearrange("k q i t -> k q (i t)")
                    sp.dma_start(dst, src).then_inc(qk_in[u], 16)

            for u in range(2):
                sp.wait_ge(qk_out[u], 32 * (PAIRS // 2))

            def slot_fn(b, p, u, now, nxt, prev, prev2):
                if nxt:
                    wait(sp, b_mm, 4 * b)
                    load_qk(b + 1, 1 - u)
                if prev2:
                    sp.wait_ge(x2n_ok, b - 1)
                    sp.dma_start(rows_dram[bass.ds((b - 2) * S, S), :],
                                 rows[u][:, :, :].rearrange("t a d -> t (a d)")).then_inc(rows_out[u], 16)
            run_slots(sp, slot_fn)

        @block.gpsimd
        def _(pool):
            g = nc.gpsimd
            g.memset(ident[:, :], 0.0)
            g.memset(ones[:, :], 1.0)
            g.memset(ones_bf[:, :], 1.0)
            g.memset(pick[:, :, :], 0.0)
            g.memset(power[:, :], -0.5)
            g.memset(eps[:, :], EPS)
            g.memset(seen[:, :], 0.0)
            for u in range(2):
                g.memset(maxparts[u][:, :, :, :], 0.0)
                g.memset(vpad[u][:, :, :], 0.0)
            pool.drain()
            g.affine_select(out=ident[:, :], in_=ident[:, :], compare_op=ALU.not_equal, fill=1.0,
                            base=0, pattern=[[-1, 128]], channel_multiplier=1)
            g.affine_select(out=below[:, :], in_=ones_bf[:, :], compare_op=ALU.is_gt, fill=0.0,
                            base=0, pattern=[[1, 128]], channel_multiplier=-1)
            g.iota(count[:, :], pattern=[[1, 128]], base=0, channel_multiplier=0,
                   allow_small_or_imprecise_dtypes=True)
            g.iota(token_no[:, :], pattern=[[S, 2]], base=1, channel_multiplier=1,
                   allow_small_or_imprecise_dtypes=True)
            for u in range(2):
                g.memset(vpad[u][:, :, HD:HD + 1], 1.0)
            pool.drain()
            g.tensor_copy(ident_bf[:, :], ident[:, :]).then_inc(consts, 1)
            pool.wait_ge(x_var, 1)
            g.tensor_scalar(var1[:, :], mv1[:, :, 1], EPS, None, ALU.add)
            pool.drain()
            g.tensor_tensor(rstd1[:, :], var1[:, :], power[:, :], ALU.pow).then_inc(x_rstd, 1)
            for p in range(2):
                for a in range(PARTS):
                    g.affine_select(out=pick[:, :, :], in_=pick[:, :, :], compare_op=ALU.not_equal,
                                    fill=-1.0, base=-(64 * p + HALF * a),
                                    pattern=[[-1, HALF], [0, S]], channel_multiplier=1)
                    pool.drain()
            g.memset(expert_of[:, :], 0.0)
            pool.drain()
            for e in range(1, E):
                g.affine_select(out=expert_of[:, :], in_=expert_of[:, :], compare_op=ALU.is_gt,
                                fill=float(e), base=e * PAGES, pattern=[[0, 1]], channel_multiplier=-1)
                pool.drain()
            g.tensor_copy(ident_bf[:, :], ident[:, :]).then_inc(consts, 1)

            with pool.Fori(0, PAIRS // 2) as i:
                for u in range(2):
                    pair = 2 * i + u
                    pool.wait_ge(high_ok, pair + 1)
                    g.tensor_tensor(resid[u][:, :, :], qkf[u][:, :, :], parts[u][:, 0::SLOTS, :],
                                    ALU.subtract).then_inc(resid_ok, 1)

            pool.wait_ge(obias_ready, 1)
            g.tensor_tensor(xb_all[:, :, :], x_all[:, :, :],
                            obias[:, :].unsqueeze(1).to_broadcast([128, B, D]), ALU.add).then_inc(xb_ready, 1)
            pool.wait_ge(v_ok, PAIRS)

            def slot_fn(b, p, u, now, nxt, prev, prev2):
                if nxt:
                    wait(pool, pv_mm, 4 * b)
                    g.tensor_copy(vpad[1 - u][:, :, 0:HD],
                                  v_all[:, bass.ds(b + 1, 1), :].rearrange("k o (h c) -> k (o h) c", h=HEADS)
                                  ).then_inc(vpad_ok, 1)
                if prev:
                    pool.wait_ge(x2_var, b)
                    g.tensor_tensor(var2[1 - u][:, :], mv2[1 - u][:, 1:2], eps[:, :], ALU.add)
                    pool.drain()
                    g.tensor_tensor(rstd2[1 - u][:, :], var2[1 - u][:, :], power[:, 0:1],
                                    ALU.pow).then_inc(x2_rstd, 1)
            run_slots(pool, slot_fn)

            pool.wait_ge(index_ok, 1)
            for u in range(2):
                pool.wait_ge(rows_out[u], 16 * PAIRS)

            def gather(j, u):
                g.tensor_copy(gather_at[u][:, :], from_row[:, bass.ds(j, 1)])
                pool.drain()
                g.indirect_dma_start(got[u][:, :], None, rows_dram[:, :],
                                     bass.IndirectOffsetOnAxis(gather_at[u][:, :], 0)).then_inc(gathered[u], 16)

            gather(0, 0)
            gather(1, 1)
            pool.wait_ge(in_ffn, 16 * N_IN_FFN)

            def step_fn(j, i, u, has):
                if has(0):
                    pool.wait_ge(gathered[u], 16 * (i + 1))
                    wait(pool, final_ok, j - 1)
                    e = pool.value_load(tile_expert[0:1, bass.ds(j, 1)], min_val=0, max_val=E - 1)
                    g.tensor_tensor(base[u][:, :], got[u][:, 0:D], b2_sb[:, bass.ds(e * D, D)],
                                    ALU.add).then_inc(base_ok, 1)
                if has(2):
                    pool.wait_ge(gotT_mm, j + 1)
                    pool.wait_ge(base_ok, j + 1)
                    gather(j + 2, u)
                if has(-2):
                    wait(pool, scattered[u], 16 * (i - 1))
                    pool.wait_ge(final_ok, j - 1)
                    g.tensor_copy(scatter_at[u][:, :], to_row[:, bass.ds(j - 2, 1)])
                    pool.drain()
                    g.indirect_dma_start(out, bass.IndirectOffsetOnAxis(scatter_at[u][:, :], 0),
                                         final[u][:, :], None, bounds_check=TOKENS - 1,
                                         oob_is_err=False).then_inc(scattered[u], 16)
            run_tiles(pool, step_fn)
            for u in range(2):
                pool.wait_ge(scattered[u], 16 * ((TILES - u + 1) // 2))

        @block.scalar
        def _(act):
            a = nc.scalar
            act.dma_start(w1_sb[:, :].rearrange("p (e f) -> p e f", e=E), w1.rearrange("e p f -> p e f")).then_inc(in_ffn, 16)
            act.dma_start(w2_sb[:, :].rearrange("p (g d) -> p g d", d=D), w2.rearrange("e (c p) d -> p (e c) d", p=128)).then_inc(in_ffn, 16)
            act.dma_start(b1_sb[:, :], b1.partition_broadcast(128)).then_inc(in_ffn, 16)
            act.dma_start(b2_sb[:, :], b2.partition_broadcast(128)).then_inc(in_ffn, 16)
            act.wait_ge(in_w, 160)

            def evac_T(pair, u):
                act.wait_ge(T_mm, pair + 1)
                wait(act, V_mm, pair - 1)
                a.copy(stagedT[u][:, :], bank[u][:, :]).then_inc(T_ok, 1)

            def evac_P(pair, u, half):
                act.wait_ge(P_mm, pair + 1)
                wait(act, resid_ok, pair - 1)
                a.activation(qkf[u][:, 0, :], bank[2 + u][:, 0:2 * S], ACT.Identity, bias=bq_sb[:, 0:1])
                a.activation(qkf[u][:, 1, :], bank[2 + u][:, 2 * S:4 * S], ACT.Identity,
                             bias=bk_sb[:, 0:1]).then_inc(qkf_ok, 1)
                act.wait_ge(qkf_ok, pair + 1)
                wait(act, qk_out[u], 32 * half)
                a.copy(parts[u][:, 0::SLOTS, :], qkf[u][:, :, :]).then_inc(high_ok, 1)
                act.wait_ge(V_mm, pair + 1)
                a.copy(v_all[:, bass.ds(2 * pair, 2), :].rearrange("k b d -> k (b d)"),
                       bank[4 + u][:, 0:2 * D]).then_inc(v_ok, 1)
            run_front(evac_T, evac_P)(act)

            def slot_fn(b, p, u, now, nxt, prev, prev2):
                if prev:
                    act.wait_ge(pv_mm, 4 * b)
                    wait(act, o_mm, b - 1)
                    a.copy(oT[:, :], bank[4][:, :]).then_inc(oT_ok, 1)

                def exps(f):
                    act.wait_ge(b_mm, 4 * b + f + 1)
                    wait(act, pv_mm, 4 * b + f - 3)
                    a.activation(probsT[f][:, :], bank[2 + f % 2][:, :], ACT.Exp,
                                 scale=float(HD) ** -0.5).then_inc(probs_ok, 1)
                if now:
                    exps(0)
                    exps(1)
                if prev2:
                    act.wait_ge(x2T_mm, b - 1)
                    wait(act, lg_mm, b - 2)
                    a.copy(x2T[:, :], bank[7][:, 0:S]).then_inc(x2T_ok, 1)
                if prev:
                    act.wait_ge(attT_mm, b)
                    wait(act, wo_mm, b - 1)
                    a.copy(attT[:, :], bank[6][:, 0:S]).then_inc(attT_ok, 1)
                if now:
                    exps(2)
                    exps(3)
                if nxt:
                    act.wait_ge(maxT_mm, b + 2)
                    a.copy(maxT[1 - u][:, :], bank[6][:, 0:S // 2].bitcast(bf16)).then_inc(maxT_ok, 1)
            run_slots(act, slot_fn)

            def step_fn(j, i, u, has):
                if has(1):
                    act.wait_ge(gotT_mm, j + 2)
                    wait(act, h_mm, j)
                    a.copy(gotT[1 - u][:, :], bank[6][:, 0:S]).then_inc(gotT_ok, 1)
                if has(0):
                    act.wait_ge(gate_ok, j + 1)
                    wait(act, hid_ok, j - 1)
                    a.activation(sig[u][:, :], gate[u][:, :], ACT.Sigmoid).then_inc(sig_ok, 1)
                if has(-1):
                    act.wait_ge(hidT_mm, j)
                    wait(act, y_mm, j - 2)
                    a.copy(hidT[1 - u][:, :], bank[5 - u][:, :]).then_inc(hidT_ok, 1)
            act.wait_ge(gotT_mm, 1)
            a.copy(gotT[0][:, :], bank[6][:, 0:S]).then_inc(gotT_ok, 1)
            run_tiles(act, step_fn)

        @block.vector
        def _(dve):
            v = nc.vector
            dve.wait_ge(in_x, 16)
            for b in range(B):
                v.bn_stats(stats1[:, b, :], x_all[:, b, :])
            dve.drain()
            for b in range(B):
                last = v.bn_aggr(mv1[:, b, :], stats1[:, b, :])
            last.then_inc(x_var, 1)
            dve.wait_ge(consts, 1)
            dve.wait_ge(in_w, 16 * 10)
            v.tensor_scalar(bv_cols[:, :], ones[:, :], bv_sb[:, 0:1], None, ALU.mult).then_inc(bv_ready, 1)
            dve.wait_ge(in_ctx, 16)
            dve.wait_ge(x_rstd, 1)

            def stage(pair, u):
                wait(dve, T_mm, pair - 1)
                for k in range(2):
                    b = bass.ds(2 * pair + k, 1)
                    v.tensor_scalar(staged[u][:, k, :], x_all[:, b, :].rearrange("t o d -> t (o d)"),
                                    mv1[:, b, 0:1].rearrange("t o d -> t (o d)"), rstd1[:, b],
                                    ALU.subtract, ALU.mult)
                v.tensor_copy(staged[u][:, 2:4, :], ctx_all[:, bass.ds(2 * pair, 2), :]).then_inc(staged_ok, 1)

            def split(pair, u, half):
                s = parts[u]
                dve.wait_ge(high_ok, pair + 1)
                dve.wait_ge(resid_ok, pair + 1)
                v.tensor_copy(s[:, 1::SLOTS, :], resid[u][:, :, :])
                v.tensor_copy(s[:, 3:5, :], s[:, 0:1, :].to_broadcast([128, 2, 2 * S]))
                v.tensor_copy(s[:, 8:12:3, :], s[:, 6:7, :].to_broadcast([128, 2, 2 * S]))
                dve.drain()
                v.tensor_tensor(s[:, 2:11:8, :], resid[u][:, :, :], s[:, 1::SLOTS, :], ALU.subtract
                                ).then_inc(parts_ok, 1)
                v.tensor_copy(s[:, 5:10:4, :], s[:, 1::SLOTS, :]).then_inc(parts_ok, 1)
            run_front(stage, split)(dve)
            dve.wait_ge(obias_mm, 1)
            v.tensor_tensor(obias[:, :], bank[6][:, 0:D], bo_sb[:, :], ALU.add).then_inc(obias_ready, 1)
            dve.wait_ge(xb_ready, 1)

            def slot_fn(b, p, u, now, nxt, prev, prev2):
                w = 1 - u
                if prev2:
                    dve.wait_ge(x2_rstd, b - 1)
                    v.tensor_scalar(rows[u][:, 1, :], rows[u][:, 0, :], mv2[u][:, 0:1], rstd2[u][:, 0:1],
                                    ALU.subtract, ALU.mult).then_inc(x2n_ok, 1)
                if prev:
                    dve.wait_ge(o_mm, b)
                    wait(dve, attT_mm, b - 1)
                    o = bank[5][:, :].rearrange("t (h c) -> t h c", c=32)
                    v.reciprocal(rsum[:, :], o[:, :, HD])
                    dve.drain()
                    v.tensor_tensor(att[:, :, :], o[:, :, 0:HD],
                                    rsum[:, :].unsqueeze(2).to_broadcast([128, HEADS, HD]),
                                    ALU.mult).then_inc(att_ok, 1)

                def maxes(f):
                    dve.wait_ge(a_mm, 4 * b + f + 5)
                    v.tensor_reduce(rowmax[w][:, 4 * f:4 * f + 4],
                                    bank[f % 2][:, :].rearrange("t (j k) -> t j k", j=4), X, ALU.max
                                    ).then_inc(max_ok, 1)
                if nxt:
                    maxes(0)
                if prev2:
                    dve.wait_ge(lg_mm, b - 1)
                    v.tensor_tensor(logits[:, u, :], bank[7][:, 0:E], rb_sb[:, :], ALU.add).then_inc(lg_read, 1)
                    if u == 1:
                        dve.drain()
                        for k in range(2):
                            v.max(top[:, k, :], logits[:, k, :])
                        dve.drain()
                        for k in range(2):
                            v.max_index(topi[:, k, :], top[:, k, :], logits[:, k, :])
                        dve.drain()
                        v.tensor_tensor(onehot[:, :, :], count[:, 0:E].unsqueeze(1).to_broadcast([128, 2, E]),
                                        topi[:, :, 0:1].to_broadcast([128, 2, E]), ALU.is_equal
                                        ).then_inc(onehot_ok, 1)
                if nxt:
                    maxes(1)
                    maxes(2)
                    maxes(3)
                    mp = maxparts[w]
                    top_in = rowmax[w][:, :].rearrange("t (p i) -> t p i", p=2)
                    res = maxres[w][:, :].rearrange("t (p i) -> t p i", p=2)
                    dve.drain()
                    v.tensor_copy(mp[:, :, 0, :], top_in)
                    dve.drain()
                    v.tensor_tensor(res, top_in, mp[:, :, 0, :], ALU.subtract)
                    dve.drain()
                    v.tensor_copy(mp[:, :, 1, :], res)
                    dve.drain()
                    v.tensor_tensor(mp[:, :, 2, :], res, mp[:, :, 1, :], ALU.subtract).then_inc(maxparts_ok, 1)
                if prev2 and u == 1:
                    dve.wait_ge(rank_mm, p)
                    v.tensor_tensor(ranksel[:, :, :], bank[5][:, 0:2 * E].rearrange("t (k e) -> t k e", k=2),
                                    onehot[:, :, :], ALU.mult).then_inc(rank_read, 1)
                    v.tensor_tensor(seen[:, :], seen[:, :], onehot[:, 0, :], ALU.add)
                    dve.drain()
                    v.tensor_tensor(seen[:, :], seen[:, :], onehot[:, 1, :], ALU.add)
                    v.tensor_reduce(rankf[:, :], ranksel[:, :, :], X, ALU.add)
                    dve.drain()
                    v.tensor_copy(rank[:, :], rankf[:, :])
                    dve.drain()
                    v.tensor_scalar(page[:, :], rank[:, :], 7, None, ALU.arith_shift_right)
                    v.tensor_scalar(slot_i[:, :], rank[:, :], 127, None, ALU.bitwise_and)
                    dve.drain()
                    v.scalar_tensor_tensor(pagecode[:, :], topi[:, :, 0], float(PAGES), page[:, :],
                                           ALU.mult, ALU.add)
                    v.tensor_copy(slot[:, :], slot_i[:, :])
                    dve.drain()
                    for k in range(2):
                        t = bass.ds(b - 3 + k, 1)
                        v.tensor_scalar(in_page[:, t, :].rearrange("t o q -> t (o q)"), count[:, :],
                                        pagecode[:, k:k + 1], None, ALU.is_equal)
                        v.tensor_scalar(at_slot[:, t, :].rearrange("t o q -> t (o q)"), count[:, :],
                                        slot[:, k:k + 1], token_no[:, k:k + 1], ALU.is_equal, ALU.mult)
                    dve.drain()
                    v.tensor_scalar(token_no[:, :], token_no[:, :], float(2 * S), None, ALU.add
                                    ).then_inc(routed, 1)
                if prev:
                    dve.wait_ge(wo_mm, b)
                    wait(dve, rows_out[w], 16 * (p - 1 + u))
                    v.tensor_tensor(rows[w][:, 0, :], bank[7][:, 0:D],
                                    xb_all[:, bass.ds(b - 1, 1), :].rearrange("t o d -> t (o d)"), ALU.add)
                    dve.drain()
                    v.bn_stats(stats2[:, :], rows[w][:, 0, :])
                    dve.drain()
                    v.bn_aggr(mv2[w][:, :], stats2[:, :]).then_inc(x2_var, 1)
            run_slots(dve, slot_fn)

            dve.wait_ge(table_mm, 1)
            v.tensor_copy(table[:, :], bank[0][:, 0:128])
            v.tensor_scalar(occ[:, :], bank[0][:, 0:1], 0.5, None, ALU.is_gt)
            v.tensor_scalar(occ_bf[:, :], bank[0][:, 0:1], 0.5, None, ALU.is_gt).then_inc(occ_ok, 1)
            dve.wait_ge(tileno_mm, 1)
            v.tensor_copy(tile_of[:, :], bank[1][:, 0:1])
            dve.drain()
            v.tensor_scalar(choose[:, :], count[:, 0:TILES], tile_of[:, 0:1], occ[:, 0:1],
                            ALU.is_equal, ALU.mult).then_inc(choose_ok, 1)
            dve.wait_ge(index_mm, 1)
            v.tensor_scalar(from_row[:, :], bank[2][:, 0:TILES], -1.0, 0.0, ALU.add, ALU.max)
            v.tensor_scalar(pad[:, :], bank[2][:, 0:TILES], 0.5, float(2 * TOKENS), ALU.is_lt, ALU.mult)
            v.tensor_copy(tile_expert[:, :], bank[3][0:1, 0:TILES])
            dve.drain()
            v.scalar_tensor_tensor(to_row[:, :], pad[:, :], -1.0, bank[2][:, 0:TILES], ALU.add, ALU.add
                                   ).then_inc(index_ok, 1)
            dve.wait_ge(in_ffn, 16 * N_IN_FFN)
            dve.wait_ge(index_ok, 1)

            def step_fn(j, i, u, has):
                if has(0):
                    e = dve.value_load(tile_expert[0:1, bass.ds(j, 1)], min_val=0, max_val=E - 1)
                    dve.wait_ge(h_mm, j + 1)
                    v.tensor_tensor(gate[u][:, :], bank[1 + 2 * u][:, :],
                                    b1_sb[:, bass.ds(e * (2 * F) + F, F)], ALU.add).then_inc(gate_ok, 1)
                    v.tensor_tensor(up[u][:, :], bank[2 * u][:, :],
                                    b1_sb[:, bass.ds(e * (2 * F), F)], ALU.add).then_inc(up_ok, 1)
                if has(-2):
                    dve.wait_ge(y_mm, j - 1)
                    dve.wait_ge(base_ok, j - 1)
                    wait(dve, scattered[u], 16 * (i - 1))
                    v.tensor_tensor(final[u][:, :], bank[7][:, 0:D], base[u][:, :], ALU.add).then_inc(final_ok, 1)
                if has(0):
                    dve.wait_ge(sig_ok, j + 1)
                    dve.wait_ge(up_ok, j + 1)
                    wait(dve, hidT_mm, j - 1)
                    v.tensor_tensor(hid[u][:, :], up[u][:, :], sig[u][:, :], ALU.mult).then_inc(hid_ok, 1)
            run_tiles(dve, step_fn)

        @block.tensor
        def _(pe):
            t = nc.tensor
            pe.wait_ge(consts, 1)
            pe.wait_ge(in_w, 160)

            def transposes(pair, u):
                pe.wait_ge(staged_ok, pair + 1)
                wait(pe, T_ok, pair - 1)
                for k in range(4):
                    last = t.transpose(bank[u][:, k * S:(k + 1) * S], staged[u][:, k, :], ident[:, :])
                last.then_inc(T_mm, 1)

            def project(pair, u, half):
                pe.wait_ge(T_ok, pair + 1)
                wait(pe, qkf_ok, pair - 1)
                t.matmul(bank[2 + u][:, 0:2 * S], wq_sb[:, :], stagedT[u][:, 0:2 * S], start=True, stop=True)
                t.matmul(bank[2 + u][:, 2 * S:4 * S], wk_sb[:, :], stagedT[u][:, 2 * S:4 * S],
                         start=True, stop=True).then_inc(P_mm, 1)
                wait(pe, v_ok, pair - 1)
                for k in range(2):
                    last = t.matmul(bank[4 + u][:, k * D:(k + 1) * D], stagedT[u][:, (2 + k) * S:(3 + k) * S],
                                    wv_sb[:, :], start=True, stop=True)
                last.then_inc(V_mm, 1)
            run_front(transposes, project)(pe)
            pe.wait_ge(bv_ready, 1)
            t.matmul(bank[6][:, 0:D], bv_cols[:, :], wo_sb[:, :], start=True, stop=True).then_inc(obias_mm, 1)
            pe.wait_ge(qkf_ok, PAIRS)
            pe.wait_ge(v_ok, PAIRS)
            pe.wait_ge(obias_ready, 1)
            pe.wait_ge(consts, 2)

            def slot_fn(b, p, u, now, nxt, prev, prev2):
                w = 1 - u

                def scores_for_max(f):
                    if f == 0:
                        pe.wait_ge(qk_in[w], 32 * (p + 1 + u))
                    wait(pe, max_ok, 4 * b + f + 3)
                    lo = 64 * (f // 2)
                    for j in range(4):
                        i = 4 * (f % 2) + j
                        last = t.matmul(bank[f % 2][:, j * S:(j + 1) * S], qk[w][lo:lo + ROWS, 0, i, :],
                                        qk[w][lo:lo + ROWS, 1, i, :], start=True, stop=True)
                    last.then_inc(a_mm, 1)

                def scores_T(f):
                    if f == 0:
                        pe.wait_ge(maxT_ok, b + 1)
                    wait(pe, probs_ok, 4 * b + f - 1)
                    lo = 64 * (f // 2)
                    for j in range(4):
                        i = 4 * (f % 2) + j
                        dst = bank[2 + f % 2][:, j * S:(j + 1) * S]
                        t.matmul(dst, qk[u][lo:lo + ROWS, 1, i, :], qk[u][lo:lo + ROWS, 0, i, :],
                                 start=True, stop=False)
                        last = t.matmul(dst, pick[lo:lo + ROWS, i, :], maxT[u][lo:lo + ROWS, :],
                                        start=False, stop=True)
                    last.then_inc(b_mm, 1)

                def times_v(f):
                    pe.wait_ge(probs_ok, 4 * b + f + 1)
                    if f == 0:
                        pe.wait_ge(vpad_ok, b + 1)
                    for j in range(4):
                        last = t.matmul(bank[4][32 * j:32 * j + 32, f * S:(f + 1) * S], vpad[u][:, 4 * f + j, :],
                                        probsT[f][:, j * S:(j + 1) * S], start=True, stop=True)
                    last.then_inc(pv_mm, 1)

                if now:
                    scores_T(0)
                if prev:
                    pe.wait_ge(oT_ok, b)
                    if u == 0:
                        wait(pe, rank_read, p - 1)
                    for f in range(4):
                        last = t.transpose(bank[5][:, f * S:(f + 1) * S], oT[:, f * S:(f + 1) * S], ident[:, :])
                    last.then_inc(o_mm, 1)
                if now:
                    scores_T(1)
                if prev2:
                    pe.wait_ge(x2n_ok, b - 1)
                    t.transpose(bank[7][:, 0:S], rows[u][:, 1, :], ident[:, :]).then_inc(x2T_mm, 1)
                if now:
                    times_v(0)
                if prev:
                    pe.wait_ge(att_ok, b)
                    t.transpose(bank[6][:, 0:S], att[:, :, :].rearrange("t h c -> t (h c)"),
                                ident[:, :]).then_inc(attT_mm, 1)
                if nxt:
                    scores_for_max(0)
                if prev2:
                    pe.wait_ge(x2T_ok, b - 1)
                    t.matmul(bank[7][:, 0:E], x2T[:, :], rw_sb[:, :], start=True, stop=True).then_inc(lg_mm, 1)
                if now:
                    scores_T(2)
                if nxt:
                    scores_for_max(1)
                if now:
                    scores_T(3)
                if nxt:
                    scores_for_max(2)
                if now:
                    times_v(1)
                if nxt:
                    scores_for_max(3)
                if now:
                    times_v(2)
                if prev:
                    pe.wait_ge(attT_ok, b)
                    wait(pe, lg_read, b - 1)
                    t.matmul(bank[7][:, 0:D], attT[:, :], wo_sb[:, :], start=True, stop=True).then_inc(wo_mm, 1)
                if prev2 and u == 1:
                    pe.wait_ge(onehot_ok, p)
                    r = bank[5]
                    t.matmul(r[:, 0:E], below[:, :], onehot[:, 0, :], start=True, stop=False)
                    t.matmul(r[:, 0:E], ones_bf[:, :], seen[:, :], start=False, stop=True)
                    t.matmul(r[:, E:2 * E], below[:, :], onehot[:, 1, :], start=True, stop=False)
                    t.matmul(r[:, E:2 * E], ones_bf[:, :], onehot[:, 0, :], start=False, stop=False)
                    t.matmul(r[:, E:2 * E], ones_bf[:, :], seen[:, :], start=False, stop=True
                             ).then_inc(rank_mm, 1)
                if now:
                    times_v(3)
                if nxt:
                    pe.wait_ge(maxparts_ok, b + 2)
                    t.transpose(bank[6][:, 0:S // 2].bitcast(bf16), maxparts[w][:, :, :, :].rearrange(
                        "t p a i -> t (p a i)"), ident_bf[:, :]).then_inc(maxT_mm, 1)
            run_slots(pe, slot_fn)

            pe.wait_ge(routed, PAIRS)
            for k in range(B):
                last = t.matmul(bank[0][:, 0:128], in_page[:, k, :], at_slot[:, k, :],
                                start=(k == 0), stop=(k == B - 1))
            last.then_inc(table_mm, 1)
            pe.wait_ge(occ_ok, 1)
            t.matmul(bank[1][:, 0:1], below[:, :], occ_bf[:, :], start=True, stop=True).then_inc(tileno_mm, 1)
            pe.wait_ge(choose_ok, 1)
            t.matmul(bank[2][:, 0:TILES], table[:, :], choose[:, :], start=True, stop=True)
            t.matmul(bank[3][0:1, 0:TILES], expert_of[:, :], choose[:, :], start=True, stop=True).then_inc(index_mm, 1)
            pe.wait_ge(index_ok, 1)
            pe.wait_ge(in_ffn, 16 * N_IN_FFN)

            def tile_T(j, u, i):
                pe.wait_ge(gathered[u], 16 * (i + 1))
                t.transpose(bank[6][:, 0:S], got[u][:, D:2 * D], ident[:, :]).then_inc(gotT_mm, 1)

            tile_T(0, 0, 0)

            def step_fn(j, i, u, has):
                if has(0):
                    pe.wait_ge(gotT_ok, j + 1)
                    wait(pe, up_ok, j - 1)
                    e = pe.value_load(tile_expert[0:1, bass.ds(j, 1)], min_val=0, max_val=E - 1)
                    for k in range(2):
                        last = t.matmul(bank[2 * u + k][:, :], gotT[u][:, :],
                                        w1_sb[:, bass.ds(e * (2 * F) + k * F, F)], start=True, stop=True)
                    last.then_inc(h_mm, 1)
                if has(1):
                    tile_T(j + 1, 1 - u, i + u)
                if has(-2):
                    pe.wait_ge(hidT_ok, j - 1)
                    wait(pe, final_ok, j - 2)
                    e2 = pe.value_load(tile_expert[0:1, bass.ds(j - 2, 1)], min_val=0, max_val=E - 1)
                    for c in range(4):
                        last = t.matmul(bank[7][:, 0:D], hidT[u][:, c * 128:(c + 1) * 128],
                                        w2_sb[:, bass.ds(e2 * F + c * D, D)], start=(c == 0), stop=(c == 3))
                    last.then_inc(y_mm, 1)
                if has(-1):
                    pe.wait_ge(hid_ok, j)
                    for c in range(4):
                        last = t.transpose(bank[5 - u][:, c * 128:(c + 1) * 128],
                                           hid[1 - u][:, c * 128:(c + 1) * 128], ident[:, :])
                    last.then_inc(hidT_mm, 1)
            run_tiles(pe, step_fn)


def kernel(x, ctx_1024, L0_xattn_Wq, L0_xattn_bq, L0_xattn_Wk, L0_xattn_bk, L0_xattn_Wv, L0_xattn_bv,
           L0_xattn_Wo, L0_xattn_bo, L0_ffn_router_w, L0_ffn_router_b, L0_ffn_w1, L0_ffn_b1, L0_ffn_w2,
           L0_ffn_b2):
    import numpy as np
    import concourse.bacc as bacc
    from concourse.bass_utils import run_bass_kernel_spmd

    order = np.arange(D).reshape(HEADS, HD).T.reshape(-1)
    arrays = {
        "x": x, "ctx": ctx_1024,
        "wq": np.asarray(L0_xattn_Wq)[order].T, "wk": np.asarray(L0_xattn_Wk)[order].T,
        "wv": np.asarray(L0_xattn_Wv).T, "wo": np.asarray(L0_xattn_Wo).T,
        "bq": np.asarray(L0_xattn_bq)[order].reshape(D, 1), "bk": np.asarray(L0_xattn_bk)[order].reshape(D, 1),
        "bv": np.asarray(L0_xattn_bv).reshape(D, 1), "bo": L0_xattn_bo,
        "rw": L0_ffn_router_w, "rb": L0_ffn_router_b,
        "w1": L0_ffn_w1, "b1": np.asarray(L0_ffn_b1).reshape(-1),
        "w2": L0_ffn_w2, "b2": np.asarray(L0_ffn_b2).reshape(-1),
    }
    arrays = {n: np.ascontiguousarray(a) for n, a in arrays.items()}
    nc = bacc.Bacc("TRN2", target_bir_lowering=False, num_devices=1)
    args = [nc.dram_tensor(n, a.shape, mybir.dt.from_np(a.dtype), kind="ExternalInput").ap()
            for n, a in arrays.items()]
    out = nc.dram_tensor("out", (TOKENS, D), mybir.dt.float32, kind="ExternalOutput").ap()
    xattn_ffn(nc, *args, out)
    r = run_bass_kernel_spmd(nc, [arrays], core_ids=[0])
    return r.results[0]["out"].reshape(B, S, D)
```

```python
import concourse.bass as bass
from concourse import mybir
from contextlib import ExitStack

B = 16
S = 128
D = 128
HEADS = 16
HD = D // HEADS
E = 8
F = 512
PAIRS = B // 2
TOKENS = B * S
TILES = TOKENS // S + E - 1
TOKEN_COL, EXPERT_COL = 2 * D, 2 * D + 1
WIDTH = 2 * D + 2
NO_TOKEN = 2 * TOKENS
FIRST = 4
PARTS = 3
SLOTS = 6
ROWS = SLOTS * HD
DEPTH = 64
HALF = HEADS // 2
EPS = 1e-5


def xattn_ffn(nc, x, ctx_in, columns, row_vectors, w1, b1, w2, b2, out):
    f32, bf16, f16 = mybir.dt.float32, mybir.dt.bfloat16, mybir.dt.float16
    i32, u32 = mybir.dt.int32, mybir.dt.uint32
    ALU = mybir.AluOpType
    ACT = mybir.ActivationFunctionType
    X = mybir.AxisListType.X

    qk_dram = nc.dram_tensor("qk_stacked", (PAIRS, 2, ROWS, 2, HALF, 2 * S), bf16).ap()
    tiles_dram = nc.dram_tensor("tile_rows", (TILES * S, WIDTH), f32).ap()

    with ExitStack() as stack:
        def sb(name, shape, dt=f32):
            return stack.enter_context(nc.sbuf_tensor(name, shape, dt))

        def sem(name):
            return stack.enter_context(nc.semaphore(name))

        ident = sb("ident", [128, 128])
        ident_bf = sb("ident_bf", [128, 128], bf16)
        below = sb("below", [128, 128], bf16)
        ones_bf = sb("ones_bf", [128, 128], bf16)
        ones = sb("ones", [128, 128])
        pickrow = sb("pickrow", [128, HALF])
        pick = sb("pick", [128, HALF, S], bf16)
        number = sb("number", [128, E])
        token_no = sb("token_no", [128, 2], i32)
        empty = sb("empty", [128, WIDTH])
        eps = sb("eps", [128, 1])
        power = sb("power", [128, B])

        columns_sb = sb("columns_sb", [128, 4 * D + E + 3])
        wq_sb, wk_sb, wv_sb, wo_sb = (columns_sb[:, k * D:(k + 1) * D] for k in range(4))
        rw_sb = columns_sb[:, 4 * D:4 * D + E]
        bq_sb, bk_sb, bv_sb = (columns_sb[:, 4 * D + E + k:4 * D + E + k + 1] for k in range(3))
        row_vectors_sb = sb("row_vectors_sb", [128, D + E])
        bo_sb, rb_sb = row_vectors_sb[:, 0:D], row_vectors_sb[:, D:D + E]
        w1_sb = sb("w1_sb", [128, E * 2 * F])
        b1_sb = sb("b1_sb", [128, E * 2 * F])
        w2_sb = sb("w2_sb", [128, E * F])
        b2_sb = sb("b2_sb", [128, E * D])

        x_all = sb("x_all", [128, B, D])
        ctx_all = sb("ctx_all", [128, B, D])
        v_all = sb("v_all", [128, B, D])
        xb_all = x_all
        bv_cols = sb("bv_cols", [128, 128])
        obias = sb("obias", [128, D])
        stats1 = sb("stats1", [128, B, 6])
        mv1 = sb("mv1", [128, B, 2])
        var1 = sb("var1", [128, B])
        rstd1 = sb("rstd1", [128, B])
        staged = [sb(f"staged{u}", [128, 4, D]) for u in range(2)]
        stagedT = [sb(f"stagedT{u}", [128, 4 * S]) for u in range(2)]
        qkf = [sb(f"qkf{u}", [128, 2, 2 * S]) for u in range(2)]
        resid = [sb(f"resid{u}", [128, 2, 2 * S]) for u in range(2)]
        parts = [sb(f"parts{u}", [128, 2 * SLOTS, 2 * S], bf16) for u in range(2)]

        qk = [sb(f"qk{c}", [128, 2, HALF, 2 * S], bf16) for c in range(2)]
        rowmax = [sb(f"rowmax{u}", [128, HEADS]) for u in range(2)]
        maxres = [sb(f"maxres{u}", [128, HEADS]) for u in range(2)]
        maxparts = [sb(f"maxparts{u}", [128, 2, 8, HALF], bf16) for u in range(2)]
        maxT = [sb(f"maxT{u}", [128, S], bf16) for u in range(2)]
        probsT = [sb(f"probsT{f}", [128, 4 * S]) for f in range(4)]
        vpad = [sb(f"vpad{u}", [128, HEADS, 32]) for u in range(2)]
        oT = sb("oT", [128, 4 * S])
        rsum = sb("rsum", [128, HEADS])
        att = sb("att", [128, HEADS, HD])
        attT = sb("attT", [128, S])
        rows = sb("rows", [128, 4, WIDTH])
        stats2 = sb("stats2", [128, 6])
        mv2 = [sb(f"mv2{u}", [128, 2]) for u in range(2)]
        var2 = [sb(f"var2{u}", [128, 1]) for u in range(2)]
        rstd2 = [sb(f"rstd2{u}", [128, 1]) for u in range(2)]
        x2T = sb("x2T", [128, S])

        logits = sb("logits", [128, 2, E])
        top = sb("top", [128, 2, 8])
        topi = sb("topi", [128, 2, 8], u32)
        onehot = sb("onehot", [128, 2, E], bf16)
        seen = sb("seen", [128, E], bf16)
        filled = sb("filled", [128, E])
        current = sb("current", [128, E])
        fresh = sb("fresh", [128, E])
        handed_out = sb("handed_out", [128, 1])
        room_i = sb("room_i", [128, E], i32)
        room = sb("room", [128, E])
        added = [sb(f"added{k}", [128, 4 + E]) for k in range(4)]
        grown = sb("grown", [128, E])
        in_new = sb("in_new", [128, 2, E])
        place = sb("place", [128, 2, E])
        placef = sb("placef", [128, 2])
        zero = sb("zero", [128, 2], u32)
        placei = sb("placei", [128, 2], u32)
        place_at = sb("place_at", [128, 2], u32)

        numbers = [sb(f"numbers{q}", [128, 1], u32) for q in range(4)]
        expert = [sb(f"expert{q}", [1, 1], u32) for q in range(4)]
        got = [sb(f"got{q}", [128, WIDTH]) for q in range(4)]
        gotT = [sb(f"gotT{u}", [128, S]) for u in range(2)]
        up = [sb(f"up{u}", [128, F]) for u in range(2)]
        gate = [sb(f"gate{u}", [128, F]) for u in range(2)]
        sig = [sb(f"sig{u}", [128, F]) for u in range(2)]
        hid, hidT = ([ctx_all[:, k + 4 * u:k + 4 * u + 4, :].rearrange("t b d -> t (b d)") for u in range(2)]
                     for k in (0, 8))
        base = [sb(f"base{q}", [128, D]) for q in range(4)]
        final = [sb(f"final{q}", [128, D]) for q in range(4)]

        bank = [stack.enter_context(nc.psum_tensor(f"bank{n}", [128, 512], f32)) for n in range(8)]

        in_x_first, in_x_rest, in_ctx, in_w, in_ffn = sem("in_x_first"), sem("in_x_rest"), sem("in_ctx"), sem("in_w"), sem("in_ffn")
        consts = sem("consts")
        x_var, x_rstd = sem("x_var"), sem("x_rstd")
        obias_mm, bv_ready, obias_ready, xb_ready = sem("obias_mm"), sem("bv_ready"), sem("obias_ready"), sem("xb_ready")
        staged_ok, T_mm, T_ok = sem("staged_ok"), sem("T_mm"), sem("T_ok")
        P_mm, V_mm = sem("P_mm"), sem("V_mm")
        qkf_ok, high_ok, v_ok = sem("qkf_ok"), sem("high_ok"), sem("v_ok")
        resid_ok, parts_ok = sem("resid_ok"), sem("parts_ok")
        qk_out = [sem("qk_out0"), sem("qk_out1")]
        qk_in = sem("qk_in")
        a_mm, max_ok, maxparts_ok, maxT_mm, maxT_ok = (
            sem(n) for n in ("a_mm", "max_ok", "maxparts_ok", "maxT_mm", "maxT_ok"))
        b_mm, probs_ok, vpad_ok, pv_mm, oT_ok, o_mm, att_ok, attT_mm, attT_ok, wo_mm = (
            sem(n) for n in ("b_mm", "probs_ok", "vpad_ok", "pv_mm", "oT_ok", "o_mm", "att_ok",
                             "attT_mm", "attT_ok", "wo_mm"))
        x2_var, x2_rstd, x2n_ok, x2T_mm, x2T_ok, lg_mm, lg_read = (
            sem(n) for n in ("x2_var", "x2_rstd", "x2n_ok", "x2T_mm", "x2T_ok", "lg_mm", "lg_read"))
        onehot_ok, rank_mm, rank_read, routed = (
            sem(n) for n in ("onehot_ok", "rank_mm", "rank_read", "routed"))
        tiles_empty = sem("tiles_empty")
        placed = [sem("placed0"), sem("placed1")]
        loaded = [sem(f"loaded{q}") for q in range(4)]
        scattered = [sem(f"scattered{q}") for q in range(4)]
        gotT_mm, gotT_ok, h_mm, gate_ok, up_ok, sig_ok, hid_ok, hidT_mm, hidT_ok, y_mm, base_ok, final_ok = (
            sem(n) for n in ("gotT_mm", "gotT_ok", "h_mm", "gate_ok", "up_ok", "sig_ok", "hid_ok",
                             "hidT_mm", "hidT_ok", "y_mm", "base_ok", "final_ok"))
        expert_ok = sem("expert_ok")

        N_IN_FFN = 2 + 2 * E

        def wait(eng, s, value):
            if isinstance(value, int) and value <= 0:
                return
            eng.wait_ge(s, value)

        def run_front(eng, ahead, step, depth=1):
            for k in range(depth):
                ahead(k, k % 2)
            for k in range(2):
                ahead(k + depth, (k + depth) % 2)
                step(k, k % 2, 0)
            with eng.Fori(1, PAIRS // 2 - 1) as i:
                for u in range(2):
                    ahead(2 * i + u + depth, (u + depth) % 2)
                    step(2 * i + u, u, i)
            for k in range(PAIRS - 2, PAIRS):
                if k + depth < PAIRS:
                    ahead(k + depth, (k + depth) % 2)
                step(k, k % 2, k // 2)

        def run_slots(eng, slot_fn):
            def peeled(b):
                slot_fn(b, b // 2, b % 2, b // 2 % 2, 0 <= b < B, b + 1 < B, 1 <= b <= B, 2 <= b <= B + 1)
            for b in range(-1, 4):
                peeled(b)
            with eng.Fori(1, B // 4 - 1) as i:
                for k in range(4):
                    slot_fn(4 * i + k, 2 * i + k // 2, k % 2, k // 2, True, True, True, True)
            for b in range(B - 4, B + 2):
                peeled(b)

        def run_tiles(eng, step_fn):
            def peeled(j):
                step_fn(j, j // 4, j % 4, lambda k: 0 <= j + k < TILES)
            for j in range(4):
                peeled(j)
            with eng.Fori(1, (TILES - 3) // 4) as i:
                for q in range(4):
                    step_fn(4 * i + q, i, q, lambda k: True)
            for j in range(4 * ((TILES - 3) // 4), TILES + 2):
                peeled(j)

        block = stack.enter_context(nc.Block())

        @block.sync
        def _(sp):
            sp.dma_start(x_all[:, 0:FIRST, :], x[0:FIRST, :, :].rearrange("b t d -> t b d")).then_inc(in_x_first, 16)
            sp.dma_start(x_all[:, FIRST:B, :], x[FIRST:B, :, :].rearrange("b t d -> t b d")).then_inc(in_x_rest, 16)

            def write_parts(pair, u):
                sp.wait_ge(parts_ok, 2 * pair + 2)
                dst = qk_dram[bass.ds(pair, 1), :, :, :, :, :].rearrange(
                    "o q (r d) p i t -> (d p i) (o q r) t", r=SLOTS)
                sp.dma_start(dst, parts[u][:, :, :]).then_inc(qk_out[u], 16)
            def load_qk(pair, c):
                for h in range(2):
                    src = qk_dram[bass.ds(pair, 1), :, :, h, :, :].rearrange("o q k i t -> k (o q) (i t)")
                    dst = qk[c][64 * h:64 * h + ROWS, :, :, :].rearrange("k q i t -> k q (i t)")
                    sp.dma_start(dst, src).then_inc(qk_in, 16)

            def load_expert(e):
                sp.dma_start(w1_sb[:, bass.ds(e * (2 * F), 2 * F)],
                             w1[bass.ds(e, 1), :, :].rearrange("o p f -> (o p) f")).then_inc(in_ffn, 16)
                sp.dma_start(w2_sb[:, bass.ds(e * F, F)].rearrange("p (c d) -> p c d", d=D),
                             w2[bass.ds(e, 1), :, :].rearrange("o (c p) d -> p (o c) d", p=128)
                             ).then_inc(in_ffn, 16)

            sp.wait_ge(consts, 1)
            sp.dma_start(tiles_dram.rearrange("(j s) w -> s j w", s=S),
                         empty[:, :].unsqueeze(1).to_broadcast([S, TILES, WIDTH])).then_inc(tiles_empty, 16)
            for u in range(2):
                write_parts(u, u)
            sp.wait_ge(qk_out[0], 16)
            load_qk(0, 0)
            with sp.Fori(1, PAIRS // 2) as i:
                for u in range(2):
                    write_parts(2 * i + u, u)
            for u in range(2):
                sp.wait_ge(qk_out[u], 16 * (PAIRS // 2))

            def slot_fn(b, p, u, c, now, nxt, prev, prev2):
                if now and u == 0 and not (isinstance(p, int) and p == PAIRS - 1):
                    sp.wait_ge(qk_in, 32 * (p + 1))
                    wait(sp, b_mm, 4 * b)
                    load_qk(p + 1, 1 - c)
                if now and u == 1:
                    load_expert(p)
            run_slots(sp, slot_fn)

            def load_tile(j, q):
                sp.dma_start(got[q][:, :], tiles_dram[bass.ds(j * S, S), :]).then_inc(loaded[q], 16)

            for k in range(2):
                sp.wait_ge(placed[k], 16 * PAIRS)
            for q in range(3):
                load_tile(q, q)

            def step_fn(j, i, q, has):
                if has(3):
                    wait(sp, gotT_mm, j)
                    wait(sp, base_ok, j)
                    load_tile(j + 3, (q + 3) % 4)
            run_tiles(sp, step_fn)

        @block.gpsimd
        def _(pool):
            g = nc.gpsimd
            g.memset(ident[:, :], 0.0)
            g.memset(power[:, :], -0.5)
            g.memset(empty[:, :], 0.0)
            pool.drain()
            g.affine_select(out=ident[:, :], in_=ident[:, :], compare_op=ALU.not_equal, fill=1.0,
                            base=0, pattern=[[-1, 128]], channel_multiplier=1)
            g.memset(ones[:, :], 1.0)
            pool.drain()
            g.memset(empty[:, TOKEN_COL:TOKEN_COL + 1].bitcast(u32), NO_TOKEN).then_inc(consts, 1)
            for k, (lo, hi) in enumerate(((0, FIRST), (FIRST, B))):
                pool.wait_ge(x_var, k + 1)
                g.tensor_scalar(var1[:, lo:hi], mv1[:, lo:hi, 1], EPS, None, ALU.add)
                pool.drain()
                g.tensor_tensor(rstd1[:, lo:hi], var1[:, lo:hi], power[:, lo:hi], ALU.pow).then_inc(x_rstd, 1)

            g.memset(ones_bf[:, :], 1.0)
            g.memset(pickrow[:, :], 0.0)
            g.memset(eps[:, :], EPS)
            g.memset(seen[:, :], 0.0)
            for t in (filled, current, handed_out, *added):
                g.memset(t[:, :], 0.0)
            g.memset(zero[:, :], 0)
            for c in range(2):
                g.memset(qk[c][:, :, :, :], 0.0)
            for u in range(2):
                g.memset(maxparts[u][:, :, :, :], 0.0)
                g.memset(vpad[u][:, :, :], 0.0)
            pool.drain()
            g.affine_select(out=below[:, :], in_=ones_bf[:, :], compare_op=ALU.is_gt, fill=0.0,
                            base=0, pattern=[[1, 128]], channel_multiplier=-1)
            g.iota(number[:, :], pattern=[[1, E]], base=0, channel_multiplier=0,
                   allow_small_or_imprecise_dtypes=True)
            g.iota(token_no[:, :], pattern=[[S, 2]], base=0, channel_multiplier=1)
            for u in range(2):
                g.memset(vpad[u][:, :, HD:HD + 1], 1.0)
            for h in range(2):
                for a in range(PARTS):
                    g.affine_select(out=pickrow[:, :], in_=pickrow[:, :], compare_op=ALU.not_equal,
                                    fill=-1.0, base=-(64 * h + HALF * a),
                                    pattern=[[-1, HALF]], channel_multiplier=1)
                    pool.drain()
            g.tensor_copy(pick[:, :, :], pickrow[:, :].unsqueeze(2).to_broadcast([128, HALF, S]))
            g.tensor_copy(ident_bf[:, :], ident[:, :]).then_inc(consts, 1)

            with pool.Fori(0, PAIRS // 2) as i:
                for u in range(2):
                    pair = 2 * i + u
                    pool.wait_ge(high_ok, pair + 1)
                    g.tensor_tensor(resid[u][:, :, :], qkf[u][:, :, :], parts[u][:, 0::SLOTS, :],
                                    ALU.subtract).then_inc(resid_ok, 1)

            pool.wait_ge(obias_ready, 1)
            pool.wait_ge(v_ok, PAIRS)

            def scatter_rows(q, c):
                pool.wait_ge(routed, q + 1)
                g.tensor_tensor(place_at[:, :], placei[:, :], zero[:, :], ALU.add)
                pool.drain()
                for k in range(2):
                    g.indirect_dma_start(tiles_dram[:, :], bass.IndirectOffsetOnAxis(place_at[:, k:k + 1], 0),
                                         rows[:, 2 * c + k, :], None).then_inc(placed[k], 16)

            def slot_fn(b, p, u, c, now, nxt, prev, prev2):
                if prev:
                    pool.wait_ge(x2_var, b)
                    g.tensor_tensor(var2[1 - u][:, :], mv2[1 - u][:, 1:2], eps[:, :], ALU.add)
                    pool.drain()
                    g.tensor_tensor(rstd2[1 - u][:, :], var2[1 - u][:, :], power[:, 0:1],
                                    ALU.pow).then_inc(x2_rstd, 1)
                if nxt:
                    wait(pool, pv_mm, 4 * b)
                    g.tensor_copy(vpad[1 - u][:, :, 0:HD],
                                  v_all[:, bass.ds(b + 1, 1), :].rearrange("k o (h c) -> k (o h) c", h=HEADS)
                                  ).then_inc(vpad_ok, 1)
                if now:
                    xb = xb_all[:, bass.ds(b, 1), :].rearrange("t o d -> t (o d)")
                    g.tensor_tensor(xb, xb, obias[:, :], ALU.add).then_inc(xb_ready, 1)
                if prev2 and u == 0 and not (isinstance(p, int) and p < 2):
                    scatter_rows(p - 2, c)
            pool.wait_ge(tiles_empty, 16)
            run_slots(pool, slot_fn)
            scatter_rows(PAIRS - 1, (PAIRS - 1) % 2)
            pool.wait_ge(in_ffn, 16 * N_IN_FFN)

            def note_expert(j, i, q, used):
                pool.wait_ge(loaded[q], 16 * (i + 1))
                wait(pool, y_mm, used)
                g.tensor_tensor(expert[q][:, :], got[q][0:1, EXPERT_COL:WIDTH].bitcast(u32), zero[0:1, 0:1],
                                ALU.add).then_inc(expert_ok, 1)

            note_expert(0, 0, 0, 0)

            def step_fn(j, i, q, has):
                if has(1):
                    note_expert(j + 1, i + (q + 1) // 4, (q + 1) % 4, j - 2)
                if has(0):
                    wait(pool, scattered[q], 16 * i)
                    pool.wait_ge(expert_ok, j + 1)
                    g.tensor_tensor(numbers[q][:, :], got[q][:, TOKEN_COL:EXPERT_COL].bitcast(u32), zero[:, 0:1],
                                    ALU.add)
                    e = pool.value_load(got[q][0:1, EXPERT_COL:WIDTH].bitcast(i32), min_val=0, max_val=E - 1)
                    wait(pool, base_ok, j - 1)
                    wait(pool, final_ok, j - 1)
                    g.tensor_tensor(base[q][:, :], got[q][:, 0:D], b2_sb[:, bass.ds(e * D, D)],
                                    ALU.add).then_inc(base_ok, 1)
                elif has(-2):
                    pool.wait_ge(final_ok, j - 1)
                if has(-2):
                    k = (q - 2) % 4
                    g.indirect_dma_start(out, bass.IndirectOffsetOnAxis(numbers[k][:, :], 0),
                                         final[k][:, :], None, bounds_check=TOKENS - 1,
                                         oob_is_err=False).then_inc(scattered[k], 16)
            run_tiles(pool, step_fn)
            for q in range(4):
                pool.wait_ge(scattered[q], 16 * ((TILES - q + 3) // 4))

        @block.scalar
        def _(act):
            a = nc.scalar
            act.dma_start(columns_sb[:, :], columns).then_inc(in_w, 16)
            act.dma_start(row_vectors_sb[:, :], row_vectors.partition_broadcast(128)).then_inc(in_w, 16)
            act.dma_start(ctx_all[:, :, :], ctx_in.rearrange("b t d -> t b d")).then_inc(in_ctx, 16)
            act.wait_ge(in_w, 32)

            def evac_T(pair, u):
                act.wait_ge(T_mm, pair + 1)
                wait(act, V_mm, pair - 1)
                a.copy(stagedT[u][:, :], bank[u][:, :]).then_inc(T_ok, 1)

            def evac_P(pair, u, half):
                act.wait_ge(P_mm, pair + 1)
                wait(act, resid_ok, pair - 1)
                a.activation(qkf[u][:, 0, :], bank[2 + u][:, 0:2 * S], ACT.Identity, bias=bq_sb[:, 0:1])
                a.activation(qkf[u][:, 1, :], bank[2 + u][:, 2 * S:4 * S], ACT.Identity,
                             bias=bk_sb[:, 0:1]).then_inc(qkf_ok, 1)
                act.wait_ge(qkf_ok, pair + 1)
                wait(act, qk_out[u], 16 * half)
                a.copy(parts[u][:, 0::SLOTS, :], qkf[u][:, :, :]).then_inc(high_ok, 1)
                act.wait_ge(V_mm, pair + 1)
                a.copy(v_all[:, bass.ds(2 * pair, 2), :].rearrange("k b d -> k (b d)"),
                       bank[4 + u][:, 0:2 * D]).then_inc(v_ok, 1)
            run_front(act, evac_T, evac_P)
            act.dma_start(b1_sb[:, :], b1.partition_broadcast(128)).then_inc(in_ffn, 16)
            act.dma_start(b2_sb[:, :], b2.partition_broadcast(128)).then_inc(in_ffn, 16)

            def slot_fn(b, p, u, c, now, nxt, prev, prev2):
                if prev:
                    act.wait_ge(pv_mm, 4 * b)
                    wait(act, o_mm, b - 1)
                    a.copy(oT[:, :], bank[4][:, :]).then_inc(oT_ok, 1)

                def exps(f):
                    act.wait_ge(b_mm, 4 * b + f + 1)
                    wait(act, pv_mm, 4 * b + f - 3)
                    a.activation(probsT[f][:, :], bank[2 + f % 2][:, :], ACT.Exp,
                                 scale=float(HD) ** -0.5).then_inc(probs_ok, 1)
                if now:
                    exps(0)
                    exps(1)
                if prev2:
                    act.wait_ge(x2T_mm, b - 1)
                    wait(act, lg_mm, b - 2)
                    a.copy(x2T[:, :], bank[7][:, 0:S]).then_inc(x2T_ok, 1)
                if prev:
                    act.wait_ge(attT_mm, b)
                    wait(act, wo_mm, b - 1)
                    a.copy(attT[:, :], bank[6][:, 0:S]).then_inc(attT_ok, 1)
                if now:
                    exps(2)
                    exps(3)
                if nxt:
                    act.wait_ge(maxT_mm, b + 2)
                    a.copy(maxT[1 - u][:, :], bank[6][:, 0:S // 2].bitcast(bf16)).then_inc(maxT_ok, 1)
            run_slots(act, slot_fn)

            def step_fn(j, i, q, has):
                u = q % 2
                if has(1):
                    act.wait_ge(gotT_mm, j + 2)
                    wait(act, h_mm, j)
                    a.copy(gotT[1 - u][:, :], bank[6][:, 0:S]).then_inc(gotT_ok, 1)
                if has(0):
                    act.wait_ge(gate_ok, j + 1)
                    wait(act, hid_ok, j - 1)
                    a.activation(sig[u][:, :], gate[u][:, :], ACT.Sigmoid).then_inc(sig_ok, 1)
                if has(-1):
                    act.wait_ge(hidT_mm, j)
                    wait(act, y_mm, j - 2)
                    a.copy(hidT[1 - u][:, :], bank[5 - u][:, :]).then_inc(hidT_ok, 1)
            act.wait_ge(gotT_mm, 1)
            a.copy(gotT[0][:, :], bank[6][:, 0:S]).then_inc(gotT_ok, 1)
            run_tiles(act, step_fn)

        @block.vector
        def _(dve):
            v = nc.vector
            for landed, batches in ((in_x_first, range(FIRST)), (in_x_rest, range(FIRST, B))):
                dve.wait_ge(landed, 16)
                for b in batches:
                    v.bn_stats(stats1[:, b, :], x_all[:, b, :])
                dve.drain()
                for b in batches:
                    last = v.bn_aggr(mv1[:, b, :], stats1[:, b, :])
                last.then_inc(x_var, 1)
            dve.wait_ge(consts, 1)
            dve.wait_ge(in_w, 32)
            v.tensor_scalar(bv_cols[:, :], ones[:, :], bv_sb[:, 0:1], None, ALU.mult).then_inc(bv_ready, 1)
            dve.wait_ge(in_ctx, 16)
            dve.wait_ge(x_rstd, 1)

            def stage(pair, u):
                wait(dve, T_mm, pair - 1)
                if isinstance(pair, int) and 2 * pair == FIRST:
                    dve.wait_ge(x_rstd, 2)
                for k in range(2):
                    b = bass.ds(2 * pair + k, 1)
                    v.tensor_scalar(staged[u][:, k, :], x_all[:, b, :].rearrange("t o d -> t (o d)"),
                                    mv1[:, b, 0:1].rearrange("t o d -> t (o d)"), rstd1[:, b],
                                    ALU.subtract, ALU.mult)
                v.tensor_copy(staged[u][:, 2:4, :], ctx_all[:, bass.ds(2 * pair, 2), :]).then_inc(staged_ok, 1)

            def split(pair, u, half):
                s = parts[u]
                dve.wait_ge(high_ok, pair + 1)
                dve.wait_ge(resid_ok, pair + 1)
                v.tensor_copy(s[:, 1::SLOTS, :], resid[u][:, :, :])
                v.tensor_copy(s[:, 3:5, :], s[:, 0:1, :].to_broadcast([128, 2, 2 * S]))
                v.tensor_copy(s[:, 8:12:3, :], s[:, 6:7, :].to_broadcast([128, 2, 2 * S]))
                dve.drain()
                v.tensor_tensor(s[:, 2:11:8, :], resid[u][:, :, :], s[:, 1::SLOTS, :], ALU.subtract
                                ).then_inc(parts_ok, 1)
                v.tensor_copy(s[:, 5:10:4, :], s[:, 1::SLOTS, :]).then_inc(parts_ok, 1)
            run_front(dve, stage, split, depth=2)
            dve.wait_ge(obias_mm, 1)
            v.tensor_tensor(obias[:, :], bank[6][:, 0:D], bo_sb[:, :], ALU.add).then_inc(obias_ready, 1)
            def slot_fn(b, p, u, c, now, nxt, prev, prev2):
                w = 1 - u
                last_row = rows[:, 2 * c if u else 2 * (1 - c) + 1, :]
                if prev2:
                    dve.wait_ge(x2_rstd, b - 1)
                    row = rows[:, 2 * (1 - c) + u, :]
                    v.tensor_scalar(row[:, D:2 * D], row[:, 0:D], mv2[u][:, 0:1], rstd2[u][:, 0:1],
                                    ALU.subtract, ALU.mult).then_inc(x2n_ok, 1)
                if prev:
                    dve.wait_ge(o_mm, b)
                    wait(dve, attT_mm, b - 1)
                    o = bank[5][:, :].rearrange("t (h c) -> t h c", c=32)
                    v.reciprocal(rsum[:, :], o[:, :, HD])
                    dve.drain()
                    v.tensor_tensor(att[:, :, :], o[:, :, 0:HD],
                                    rsum[:, :].unsqueeze(2).to_broadcast([128, HEADS, HD]),
                                    ALU.mult).then_inc(att_ok, 1)

                def maxes(f):
                    dve.wait_ge(a_mm, 4 * b + f + 5)
                    v.tensor_reduce(rowmax[w][:, 4 * f:4 * f + 4],
                                    bank[f % 2][:, :].rearrange("t (j k) -> t j k", j=4), X, ALU.max
                                    ).then_inc(max_ok, 1)
                if nxt:
                    maxes(0)
                if prev2:
                    dve.wait_ge(lg_mm, b - 1)
                    v.tensor_tensor(logits[:, u, :], bank[7][:, 0:E], rb_sb[:, :], ALU.add).then_inc(lg_read, 1)
                    if u == 1:
                        dve.drain()
                        for k in range(2):
                            v.max(top[:, k, :], logits[:, k, :])
                        dve.drain()
                        for k in range(2):
                            v.max_index(topi[:, k, :], top[:, k, :], logits[:, k, :])
                        dve.drain()
                        v.tensor_tensor(onehot[:, :, :], number[:, :].unsqueeze(1).to_broadcast([128, 2, E]),
                                        topi[:, :, 0:1].to_broadcast([128, 2, E]), ALU.is_equal
                                        ).then_inc(onehot_ok, 1)
                if nxt:
                    maxes(1)
                    maxes(2)
                    maxes(3)
                    mp = maxparts[w]
                    top_in = rowmax[w][:, :].rearrange("t (p i) -> t p i", p=2)
                    res = maxres[w][:, :].rearrange("t (p i) -> t p i", p=2)
                    dve.drain()
                    v.tensor_copy(mp[:, :, 0, :], top_in)
                    dve.drain()
                    v.tensor_tensor(res, top_in, mp[:, :, 0, :], ALU.subtract)
                    dve.drain()
                    v.tensor_copy(mp[:, :, 1, :], res)
                    dve.drain()
                    v.tensor_tensor(mp[:, :, 2, :], res, mp[:, :, 1, :], ALU.subtract).then_inc(maxparts_ok, 1)
                if prev2 and u == 1:
                    dve.wait_ge(rank_mm, p)
                    ranks = bank[5][:, 0:2 * E].rearrange("t (k e) -> t k e", k=2)
                    over_pair = lambda a: a[:, :].unsqueeze(1).to_broadcast([128, 2, E])
                    v.tensor_scalar(room_i[:, :], bank[5][:, 2 * E:3 * E], float(S - 1), None, ALU.add)
                    v.tensor_tensor(in_new[:, :, :], ranks, over_pair(filled), ALU.is_ge)
                    v.tensor_copy(rows[:, 2 * (1 - c):2 * (1 - c) + 2, TOKEN_COL:TOKEN_COL + 1].bitcast(u32),
                                  token_no[:, :].unsqueeze(2))
                    v.tensor_copy(rows[:, 2 * (1 - c):2 * (1 - c) + 2, EXPERT_COL:EXPERT_COL + 1].bitcast(u32),
                                  topi[:, :, 0:1])
                    dve.drain()
                    v.tensor_scalar(room_i[:, :], room_i[:, :], -S, None, ALU.bitwise_and)
                    v.tensor_tensor(seen[:, :], seen[:, :], onehot[:, 0, :], ALU.add)
                    v.tensor_scalar(token_no[:, :], token_no[:, :], 2 * S, None, ALU.add)
                    dve.drain()
                    v.tensor_copy(room[:, :], room_i[:, :])
                    v.tensor_tensor(seen[:, :], seen[:, :], onehot[:, 1, :], ALU.add)
                    dve.drain()
                    v.tensor_tensor(added[0][:, 4:], room[:, :], filled[:, :], ALU.subtract)
                    for k in range(3):
                        dve.drain()
                        v.tensor_tensor(added[k + 1][:, 4:], added[k][:, 4:],
                                        added[k][:, 4 - (1 << k):4 + E - (1 << k)], ALU.add)
                    v.tensor_scalar(grown[:, :], added[0][:, 4:], 0.0, None, ALU.is_gt)
                    dve.drain()
                    v.scalar_tensor_tensor(fresh[:, :], added[3][:, 4:], handed_out[:, 0:1], room[:, :],
                                           ALU.add, ALU.subtract)
                    dve.drain()
                    v.tensor_tensor(fresh[:, :], fresh[:, :], current[:, :], ALU.subtract)
                    v.tensor_copy(filled[:, :], room[:, :])
                    v.tensor_tensor(handed_out[:, :], handed_out[:, :], added[3][:, 3 + E:4 + E], ALU.add)
                    dve.drain()
                    v.tensor_tensor(in_new[:, :, :], in_new[:, :, :], over_pair(fresh), ALU.mult)
                    v.tensor_tensor(place[:, :, :], ranks, over_pair(current), ALU.add).then_inc(rank_read, 1)
                    v.tensor_tensor(grown[:, :], fresh[:, :], grown[:, :], ALU.mult)
                    dve.drain()
                    v.tensor_tensor(place[:, :, :], place[:, :, :], in_new[:, :, :], ALU.add)
                    v.tensor_tensor(current[:, :], current[:, :], grown[:, :], ALU.add)
                    dve.drain()
                    v.tensor_tensor(place[:, :, :], place[:, :, :], onehot[:, :, :], ALU.mult)
                    dve.drain()
                    wait(dve, placed[0], 16 * (p - 1))
                    wait(dve, placed[1], 16 * (p - 1))
                    v.tensor_reduce(placef[:, :], place[:, :, :], X, ALU.add)
                    dve.drain()
                    v.tensor_copy(placei[:, :], placef[:, :]).then_inc(routed, 1)
                if prev:
                    dve.wait_ge(wo_mm, b)
                    dve.wait_ge(xb_ready, b)
                    v.tensor_tensor(last_row[:, 0:D], bank[7][:, 0:D],
                                    xb_all[:, bass.ds(b - 1, 1), :].rearrange("t o d -> t (o d)"), ALU.add)
                    dve.drain()
                    v.bn_stats(stats2[:, :], last_row[:, 0:D])
                    dve.drain()
                    v.bn_aggr(mv2[w][:, :], stats2[:, :]).then_inc(x2_var, 1)
            run_slots(dve, slot_fn)
            dve.wait_ge(in_ffn, 16 * N_IN_FFN)
            dve.wait_ge(expert_ok, 1)

            def step_fn(j, i, q, has):
                u = q % 2
                if has(0):
                    e = dve.value_load(expert[q][0:1, 0:1].bitcast(i32), min_val=0, max_val=E - 1)
                    dve.wait_ge(h_mm, j + 1)
                    v.tensor_tensor(gate[u][:, :], bank[1 + 2 * u][:, :],
                                    b1_sb[:, bass.ds(e * (2 * F) + F, F)], ALU.add).then_inc(gate_ok, 1)
                    v.tensor_tensor(up[u][:, :], bank[2 * u][:, :],
                                    b1_sb[:, bass.ds(e * (2 * F), F)], ALU.add).then_inc(up_ok, 1)
                if has(-2):
                    k = (q - 2) % 4
                    dve.wait_ge(y_mm, j - 1)
                    dve.wait_ge(base_ok, j - 1)
                    v.tensor_tensor(final[k][:, :], bank[7][:, 0:D], base[k][:, :], ALU.add).then_inc(final_ok, 1)
                if has(0):
                    if has(1):
                        dve.wait_ge(expert_ok, j + 2)
                    dve.wait_ge(sig_ok, j + 1)
                    dve.wait_ge(up_ok, j + 1)
                    wait(dve, hidT_mm, j - 1)
                    v.tensor_tensor(hid[u][:, :], up[u][:, :], sig[u][:, :], ALU.mult).then_inc(hid_ok, 1)
            run_tiles(dve, step_fn)

        @block.tensor
        def _(pe):
            t = nc.tensor
            pe.wait_ge(consts, 1)
            pe.wait_ge(in_w, 32)

            def transposes(pair, u):
                pe.wait_ge(staged_ok, pair + 1)
                wait(pe, T_ok, pair - 1)
                for k in range(4):
                    last = t.transpose(bank[u][:, k * S:(k + 1) * S], staged[u][:, k, :], ident[:, :])
                last.then_inc(T_mm, 1)

            def project(pair, u, half):
                pe.wait_ge(T_ok, pair + 1)
                wait(pe, qkf_ok, pair - 1)
                t.matmul(bank[2 + u][:, 0:2 * S], wq_sb[:, :], stagedT[u][:, 0:2 * S], start=True, stop=True)
                t.matmul(bank[2 + u][:, 2 * S:4 * S], wk_sb[:, :], stagedT[u][:, 2 * S:4 * S],
                         start=True, stop=True).then_inc(P_mm, 1)
                wait(pe, v_ok, pair - 1)
                for k in range(2):
                    last = t.matmul(bank[4 + u][:, k * D:(k + 1) * D], stagedT[u][:, (2 + k) * S:(3 + k) * S],
                                    wv_sb[:, :], start=True, stop=True)
                last.then_inc(V_mm, 1)
            run_front(pe, transposes, project)
            pe.wait_ge(bv_ready, 1)
            t.matmul(bank[6][:, 0:D], bv_cols[:, :], wo_sb[:, :], start=True, stop=True).then_inc(obias_mm, 1)
            pe.wait_ge(qkf_ok, PAIRS)
            pe.wait_ge(v_ok, PAIRS)
            pe.wait_ge(obias_ready, 1)
            pe.wait_ge(consts, 2)

            def slot_fn(b, p, u, c, now, nxt, prev, prev2):
                w = 1 - u
                this_qk = qk[c][:, :, :, u * S:(u + 1) * S]
                next_qk = qk[c if u == 0 else 1 - c][:, :, :, w * S:(w + 1) * S]

                def scores_for_max(f):
                    if f == 0 and u == 1:
                        pe.wait_ge(qk_in, 32 * (p + 2))
                    wait(pe, max_ok, 4 * b + f + 3)
                    lo = 64 * (f // 2)
                    for j in range(4):
                        i = 4 * (f % 2) + j
                        last = t.matmul(bank[f % 2][:, j * S:(j + 1) * S], next_qk[lo:lo + DEPTH, 0, i, :],
                                        next_qk[lo:lo + DEPTH, 1, i, :], start=True, stop=True)
                    last.then_inc(a_mm, 1)

                def scores_T(f):
                    if f == 0:
                        pe.wait_ge(maxT_ok, b + 1)
                    wait(pe, probs_ok, 4 * b + f - 1)
                    lo = 64 * (f // 2)
                    for j in range(4):
                        i = 4 * (f % 2) + j
                        dst = bank[2 + f % 2][:, j * S:(j + 1) * S]
                        t.matmul(dst, this_qk[lo:lo + DEPTH, 1, i, :], this_qk[lo:lo + DEPTH, 0, i, :],
                                 start=True, stop=False)
                        last = t.matmul(dst, pick[lo:lo + DEPTH, i, :], maxT[u][lo:lo + DEPTH, :],
                                        start=False, stop=True)
                    last.then_inc(b_mm, 1)

                def times_v(f):
                    pe.wait_ge(probs_ok, 4 * b + f + 1)
                    if f == 0:
                        pe.wait_ge(vpad_ok, b + 1)
                    for j in range(4):
                        last = t.matmul(bank[4][32 * j:32 * j + 32, f * S:(f + 1) * S], vpad[u][:, 4 * f + j, :],
                                        probsT[f][:, j * S:(j + 1) * S], start=True, stop=True)
                    last.then_inc(pv_mm, 1)

                if now:
                    scores_T(0)
                if prev:
                    pe.wait_ge(oT_ok, b)
                    if u == 0:
                        wait(pe, rank_read, p - 1)
                    for f in range(4):
                        last = t.transpose(bank[5][:, f * S:(f + 1) * S], oT[:, f * S:(f + 1) * S], ident[:, :])
                    last.then_inc(o_mm, 1)
                if now:
                    scores_T(1)
                if prev2:
                    pe.wait_ge(x2n_ok, b - 1)
                    t.transpose(bank[7][:, 0:S], rows[:, 2 * (1 - c) + u, D:2 * D], ident[:, :]).then_inc(x2T_mm, 1)
                if now:
                    times_v(0)
                if prev:
                    pe.wait_ge(att_ok, b)
                    t.transpose(bank[6][:, 0:S], att[:, :, :].rearrange("t h c -> t (h c)"),
                                ident[:, :]).then_inc(attT_mm, 1)
                if nxt:
                    scores_for_max(0)
                if prev2:
                    pe.wait_ge(x2T_ok, b - 1)
                    t.matmul(bank[7][:, 0:E], x2T[:, :], rw_sb[:, :], start=True, stop=True).then_inc(lg_mm, 1)
                if now:
                    scores_T(2)
                if nxt:
                    scores_for_max(1)
                if now:
                    scores_T(3)
                if nxt:
                    scores_for_max(2)
                if now:
                    times_v(1)
                if nxt:
                    scores_for_max(3)
                if now:
                    times_v(2)
                if prev:
                    pe.wait_ge(attT_ok, b)
                    wait(pe, lg_read, b - 1)
                    t.matmul(bank[7][:, 0:D], attT[:, :], wo_sb[:, :], start=True, stop=True).then_inc(wo_mm, 1)
                if prev2 and u == 1:
                    pe.wait_ge(onehot_ok, p)
                    r = bank[5]
                    t.matmul(r[:, 0:E], below[:, :], onehot[:, 0, :], start=True, stop=False)
                    t.matmul(r[:, 0:E], ones_bf[:, :], seen[:, :], start=False, stop=True)
                    t.matmul(r[:, E:2 * E], below[:, :], onehot[:, 1, :], start=True, stop=False)
                    t.matmul(r[:, E:2 * E], ones_bf[:, :], onehot[:, 0, :], start=False, stop=False)
                    t.matmul(r[:, E:2 * E], ones_bf[:, :], seen[:, :], start=False, stop=True)
                    for k in range(2):
                        t.matmul(r[:, 2 * E:3 * E], ones_bf[:, :], onehot[:, k, :], start=(k == 0), stop=False)
                    t.matmul(r[:, 2 * E:3 * E], ones_bf[:, :], seen[:, :], start=False, stop=True
                             ).then_inc(rank_mm, 1)
                if now:
                    times_v(3)
                if nxt:
                    pe.wait_ge(maxparts_ok, b + 2)
                    t.transpose(bank[6][:, 0:S // 2].bitcast(bf16), maxparts[w][:, :, :, :].rearrange(
                        "t p a i -> t (p a i)"), ident_bf[:, :]).then_inc(maxT_mm, 1)
            run_slots(pe, slot_fn)

            pe.wait_ge(in_ffn, 16 * N_IN_FFN)

            def tile_T(j, q, i):
                pe.wait_ge(loaded[q], 16 * (i + 1))
                t.transpose(bank[6][:, 0:S], got[q][:, D:2 * D], ident[:, :]).then_inc(gotT_mm, 1)

            tile_T(0, 0, 0)
            pe.wait_ge(expert_ok, 1)

            def step_fn(j, i, q, has):
                u = q % 2
                if has(0):
                    e = pe.value_load(expert[q][0:1, 0:1].bitcast(i32), min_val=0, max_val=E - 1)
                    pe.wait_ge(gotT_ok, j + 1)
                    wait(pe, up_ok, j - 1)
                    for k in range(2):
                        last = t.matmul(bank[2 * u + k][:, :], gotT[u][:, :],
                                        w1_sb[:, bass.ds(e * (2 * F) + k * F, F)], start=True, stop=True)
                    last.then_inc(h_mm, 1)
                if has(1):
                    tile_T(j + 1, (q + 1) % 4, i + (q + 1) // 4)
                if has(-2):
                    e2 = pe.value_load(expert[(q - 2) % 4][0:1, 0:1].bitcast(i32), min_val=0, max_val=E - 1)
                    pe.wait_ge(hidT_ok, j - 1)
                    wait(pe, final_ok, j - 2)
                    for c in range(4):
                        last = t.matmul(bank[7][:, 0:D], hidT[u][:, c * 128:(c + 1) * 128],
                                        w2_sb[:, bass.ds(e2 * F + c * D, D)], start=(c == 0), stop=(c == 3))
                    last.then_inc(y_mm, 1)
                if has(1):
                    pe.wait_ge(expert_ok, j + 2)
                if has(-1):
                    pe.wait_ge(hid_ok, j)
                    for c in range(4):
                        last = t.transpose(bank[5 - u][:, c * 128:(c + 1) * 128],
                                           hid[1 - u][:, c * 128:(c + 1) * 128], ident[:, :])
                    last.then_inc(hidT_mm, 1)
            run_tiles(pe, step_fn)


def kernel(x, ctx_1024, L0_xattn_Wq, L0_xattn_bq, L0_xattn_Wk, L0_xattn_bk, L0_xattn_Wv, L0_xattn_bv,
           L0_xattn_Wo, L0_xattn_bo, L0_ffn_router_w, L0_ffn_router_b, L0_ffn_w1, L0_ffn_b1, L0_ffn_w2,
           L0_ffn_b2):
    import numpy as np
    import concourse.bacc as bacc
    from concourse.bass_utils import run_bass_kernel_spmd

    order = np.arange(D).reshape(HEADS, HD).T.reshape(-1)
    arrays = {
        "x": x, "ctx": ctx_1024,
        "columns": np.concatenate(
            [np.asarray(L0_xattn_Wq)[order].T, np.asarray(L0_xattn_Wk)[order].T, np.asarray(L0_xattn_Wv).T,
             np.asarray(L0_xattn_Wo).T, np.asarray(L0_ffn_router_w), np.asarray(L0_xattn_bq)[order, None],
             np.asarray(L0_xattn_bk)[order, None], np.asarray(L0_xattn_bv)[:, None]], axis=1),
        "row_vectors": np.concatenate([np.asarray(L0_xattn_bo), np.asarray(L0_ffn_router_b)]),
        "w1": L0_ffn_w1, "b1": np.asarray(L0_ffn_b1).reshape(-1),
        "w2": L0_ffn_w2, "b2": np.asarray(L0_ffn_b2).reshape(-1),
    }
    arrays = {n: np.ascontiguousarray(a) for n, a in arrays.items()}
    nc = bacc.Bacc("TRN2", target_bir_lowering=False, num_devices=1)
    args = [nc.dram_tensor(n, a.shape, mybir.dt.from_np(a.dtype), kind="ExternalInput").ap()
            for n, a in arrays.items()]
    out = nc.dram_tensor("out", (TOKENS, D), mybir.dt.float32, kind="ExternalOutput").ap()
    xattn_ffn(nc, *args, out)
    r = run_bass_kernel_spmd(nc, [arrays], core_ids=[0])
    return r.results[0]["out"].reshape(B, S, D)
```

```python
import concourse.bass as bass
from concourse import mybir
from contextlib import ExitStack

B = 16
S = 128
D = 128
HEADS = 16
HD = D // HEADS
E = 8
F = 512
PAIRS = B // 2
TOKENS = B * S
TILES = TOKENS // S + E - 1
TOKEN_COL, EXPERT_COL = 2 * D, 2 * D + 1
WIDTH = 2 * D + 2
NO_TOKEN = 2 * TOKENS
FIRST = 4
PARTS = 3
SLOTS = 6
ROWS = SLOTS * HD
DEPTH = 64
HALF = HEADS // 2
EPS = 1e-5
STEPS = 7


def xattn_ffn(nc, x, ctx_in, columns, row_vectors, w1, b1, w2, b2, out):
    f32, bf16, f16 = mybir.dt.float32, mybir.dt.bfloat16, mybir.dt.float16
    i32, u32 = mybir.dt.int32, mybir.dt.uint32
    ALU = mybir.AluOpType
    ACT = mybir.ActivationFunctionType
    X = mybir.AxisListType.X

    qk_dram = nc.dram_tensor("qk_stacked", (PAIRS, 2, ROWS, 2, HALF, 2 * S), bf16).ap()
    tiles_dram = nc.dram_tensor("tile_rows", (TILES * S, WIDTH), f32).ap()

    with ExitStack() as stack:
        def sb(name, shape, dt=f32):
            return stack.enter_context(nc.sbuf_tensor(name, shape, dt))

        def sem(name):
            return stack.enter_context(nc.semaphore(name))

        ident = sb("ident", [128, 128])
        ident_bf = sb("ident_bf", [128, 128], bf16)
        below = sb("below", [128, 128], bf16)
        ones_bf = sb("ones_bf", [128, 128], bf16)
        ones = sb("ones", [128, 128])
        pick = sb("pick", [128, HEADS], bf16)
        number = sb("number", [128, E])
        token_no = sb("token_no", [128, 2], i32)
        empty = sb("empty", [128, WIDTH])
        eps = sb("eps", [128, 1])
        power = sb("power", [128, B])

        columns_sb = sb("columns_sb", [128, 4 * D + E + 3])
        wq_sb, wk_sb, wv_sb, wo_sb = (columns_sb[:, k * D:(k + 1) * D] for k in range(4))
        rw_sb = columns_sb[:, 4 * D:4 * D + E]
        bq_sb, bk_sb, bv_sb = (columns_sb[:, 4 * D + E + k:4 * D + E + k + 1] for k in range(3))
        row_vectors_sb = sb("row_vectors_sb", [128, D + E])
        bo_sb, rb_sb = row_vectors_sb[:, 0:D], row_vectors_sb[:, D:D + E]
        w1_sb = sb("w1_sb", [128, E * 2 * F])
        b1_sb = sb("b1_sb", [128, E * 2 * F])
        w2_sb = sb("w2_sb", [128, E * F])
        b2_sb = sb("b2_sb", [128, E * D])

        x_all = sb("x_all", [128, B, D])
        ctx_all = sb("ctx_all", [128, B, D])
        v_all = sb("v_all", [128, B, D])
        xb_all = x_all
        bv_cols = sb("bv_cols", [128, 128])
        obias = sb("obias", [128, D])
        stats1 = sb("stats1", [128, B, 6])
        mv1 = sb("mv1", [128, B, 2])
        var1 = sb("var1", [128, B])
        rstd1 = sb("rstd1", [128, B])
        staged = [sb(f"staged{u}", [128, 4, D]) for u in range(2)]
        stagedT = [sb(f"stagedT{u}", [128, 4 * S]) for u in range(2)]
        qkf = [sb(f"qkf{u}", [128, 2, 2 * S]) for u in range(2)]
        resid = [sb(f"resid{u}", [128, 2, 2 * S]) for u in range(2)]
        high = [sb(f"high{u}", [128, 2, 2 * S], bf16) for u in range(2)]
        def parts(u, half):
            words = 2 * SLOTS * S
            return (w1_sb, b1_sb)[u][:, bass.ds(half * words, words)].bitcast(bf16).rearrange(
                "k (s t) -> k s t", s=2 * SLOTS)

        qk = [sb(f"qk{c}", [128, 2, HALF, 2 * S], bf16) for c in range(2)]
        rowmax = [sb(f"rowmax{u}", [128, HEADS]) for u in range(2)]
        maxres = [sb(f"maxres{u}", [128, HEADS]) for u in range(2)]
        maxparts = [sb(f"maxparts{u}", [128, 2, 8, HALF], bf16) for u in range(2)]
        maxT = [sb(f"maxT{u}", [128, S], bf16) for u in range(2)]
        probsT = [sb(f"probsT{f}", [128, 4 * S]) for f in range(4)]
        vpad = [sb(f"vpad{u}", [128, HEADS, 32]) for u in range(2)]
        oT = sb("oT", [128, 4 * S])
        rsum = sb("rsum", [128, HEADS])
        att = sb("att", [128, HEADS, HD])
        attT = sb("attT", [128, S])
        rows = sb("rows", [128, 4, WIDTH])
        x2 = [sb(f"x2_{u}", [128, 2 * D]) for u in range(2)]
        stats2 = sb("stats2", [128, 6])
        mv2 = [sb(f"mv2{u}", [128, 2]) for u in range(2)]
        var2 = [sb(f"var2{u}", [128, 1]) for u in range(2)]
        rstd2 = [sb(f"rstd2{u}", [128, 1]) for u in range(2)]
        x2T = sb("x2T", [128, S])

        logits = sb("logits", [128, 2, E])
        top = sb("top", [128, 2, 8])
        topi = sb("topi", [128, 2, 8], u32)
        onehot = sb("onehot", [128, 2, E], bf16)
        seen = sb("seen", [128, E], bf16)
        filled = sb("filled", [128, E])
        current = sb("current", [128, E])
        another = sb("another", [128, E])
        origin = sb("origin", [128, E])
        handed_out = sb("handed_out", [128, 1])
        counts = sb("counts", [128, 3 * E])
        short = sb("short", [128, E])
        one_more = sb("one_more", [128, E])
        jump = sb("jump", [128, E])
        added = [sb(f"added{k}", [128, 4 + E]) for k in range(4)]
        grown = sb("grown", [128, E])
        in_new = sb("in_new", [128, 2, E])
        place = sb("place", [128, 2, E])
        zero = sb("zero", [128, 2], u32)
        place_at = sb("place_at", [128, 2], u32)
        last_places = sb("last_places", [128, 2], u32)

        numbers = [sb(f"numbers{q}", [128, 1], u32) for q in range(4)]
        expert = [sb(f"expert{q}", [1, 1], u32) for q in range(4)]
        got = [sb(f"got{q}", [128, WIDTH]) for q in range(4)]
        gotT = [sb(f"gotT{u}", [128, S]) for u in range(2)]
        up = [sb(f"up{u}", [128, F]) for u in range(2)]
        gate = [sb(f"gate{u}", [128, F]) for u in range(2)]
        sig = [sb(f"sig{u}", [128, F]) for u in range(2)]
        hid, hidT = ([ctx_all[:, k + 4 * u:k + 4 * u + 4, :].rearrange("t b d -> t (b d)") for u in range(2)]
                     for k in (0, 8))
        base = [sb(f"base{q}", [128, D]) for q in range(4)]
        final = [sb(f"final{q}", [128, D]) for q in range(4)]

        bank = [stack.enter_context(nc.psum_tensor(f"bank{n}", [128, 512], f32)) for n in range(8)]

        in_x_first, in_x_rest, in_ctx, in_w, in_ffn = sem("in_x_first"), sem("in_x_rest"), sem("in_ctx"), sem("in_w"), sem("in_ffn")
        consts = sem("consts")
        x_var, x_rstd = sem("x_var"), sem("x_rstd")
        obias_mm, bv_ready, obias_ready, xb_ready = sem("obias_mm"), sem("bv_ready"), sem("obias_ready"), sem("xb_ready")
        staged_ok, T_mm, T_ok = sem("staged_ok"), sem("T_mm"), sem("T_ok")
        P_mm, V_mm = sem("P_mm"), sem("V_mm")
        qkf_ok, high_ok, v_ok = sem("qkf_ok"), sem("high_ok"), sem("v_ok")
        resid_ok, parts_ok = sem("resid_ok"), sem("parts_ok")
        first_out, qk_out = sem("first_out"), sem("qk_out")
        step_done, places_found = sem("step_done"), sem("places_found")
        qk_in = sem("qk_in")
        a_mm, max_ok, maxparts_ok, maxT_mm, maxT_ok = (
            sem(n) for n in ("a_mm", "max_ok", "maxparts_ok", "maxT_mm", "maxT_ok"))
        b_mm, probs_ok, vpad_ok, pv_mm, oT_ok, o_mm, att_ok, attT_mm, attT_ok, wo_mm = (
            sem(n) for n in ("b_mm", "probs_ok", "vpad_ok", "pv_mm", "oT_ok", "o_mm", "att_ok",
                             "attT_mm", "attT_ok", "wo_mm"))
        x2_var, x2_rstd, x2n_ok, x2T_mm, x2T_ok, lg_mm, lg_read = (
            sem(n) for n in ("x2_var", "x2_rstd", "x2n_ok", "x2T_mm", "x2T_ok", "lg_mm", "lg_read"))
        onehot_ok, rank_mm, rank_read, meta_ok, wo_read, row_ok, onehot_read, eps_added = (
            sem(n) for n in ("onehot_ok", "rank_mm", "rank_read", "meta_ok", "wo_read", "row_ok", "onehot_read", "eps_added"))
        tiles_empty = sem("tiles_empty")
        placed = [sem("placed0"), sem("placed1")]
        loaded = [sem(f"loaded{q}") for q in range(4)]
        scattered = [sem(f"scattered{q}") for q in range(4)]
        gotT_mm, gotT_ok, h_mm, gate_ok, up_ok, sig_ok, hid_ok, hidT_mm, hidT_ok, y_mm, base_ok, final_ok = (
            sem(n) for n in ("gotT_mm", "gotT_ok", "h_mm", "gate_ok", "up_ok", "sig_ok", "hid_ok",
                             "hidT_mm", "hidT_ok", "y_mm", "base_ok", "final_ok"))
        expert_ok = sem("expert_ok")

        N_IN_FFN = 3 * E + 1

        def wait(eng, s, value):
            if isinstance(value, int) and value <= 0:
                return
            eng.wait_ge(s, value)

        def before(b, n):
            return not isinstance(b, int) or b >= n

        def run_front(eng, ahead, step, depth=1, before_last=lambda: None):
            for k in range(depth):
                ahead(k, k % 2)
            for k in range(2):
                ahead(k + depth, (k + depth) % 2)
                step(k, k % 2, 0)
            steady = (PAIRS - depth) // 2
            with eng.Fori(1, steady) as i:
                for u in range(2):
                    ahead(2 * i + u + depth, (u + depth) % 2)
                    step(2 * i + u, u, i)
            for k in range(2 * steady, PAIRS):
                if k + depth < PAIRS:
                    ahead(k + depth, (k + depth) % 2)
                if k == PAIRS - 1:
                    before_last()
                step(k, k % 2, k // 2)

        def slot(slot_fn, b):
            slot_fn(b, b // 2, b % 2, b // 2 % 2, 0 <= b < B, b + 1 < B, 1 <= b <= B, 2 <= b <= B + 1,
                    b % 2 == 0 and b >= 4)

        def run_slots(eng, slot_fn):
            for b in range(6):
                slot(slot_fn, b)
            with eng.Fori(0, (B - 8) // 4) as i:
                for k in range(6, 10):
                    slot_fn(4 * i + k, 2 * i + k // 2, k % 2, k // 2 % 2, True, True, True, True, k % 2 == 0)
            for b in range(B - 2, B + 3):
                slot(slot_fn, b)

        def run_tiles(eng, step_fn):
            def peeled(j):
                step_fn(j, j // 4, j % 4, lambda k: 0 <= j + k < TILES)
            for j in range(4):
                peeled(j)
            with eng.Fori(1, (TILES - 3) // 4) as i:
                for q in range(4):
                    step_fn(4 * i + q, i, q, lambda k: True)
            for j in range(4 * ((TILES - 3) // 4), TILES + 2):
                peeled(j)

        def after_step(eng, p, n):
            eng.wait_ge(step_done, STEPS * (p - 2) + n)

        def hand_out(eng, e, p):
            ranks = counts[:, 0:2 * E].rearrange("t (k e) -> t k e", k=2)
            over_pair = lambda a: a[:, :].unsqueeze(1).to_broadcast([128, 2, E])
            eng.wait_ge(rank_read, p - 1)
            e.tensor_tensor(short[:, :], counts[:, 2 * E:3 * E], filled[:, :], ALU.subtract)
            e.tensor_tensor(in_new[:, :, :], ranks, over_pair(filled), ALU.subtract).then_inc(step_done, 1)
            after_step(eng, p, 1)
            e.tensor_tensor(place[:, :, :], ranks, over_pair(current), ALU.add)
            e.tensor_scalar(one_more[:, :], short[:, :], 0.0, float(S), ALU.is_gt, ALU.mult)
            e.tensor_scalar(another[:, :], short[:, :], float(S), float(S), ALU.is_gt, ALU.mult
                            ).then_inc(step_done, 1)
            after_step(eng, p, 2)
            e.tensor_tensor(added[0][:, 4:], one_more[:, :], another[:, :], ALU.add)
            e.tensor_scalar(in_new[:, :, :], in_new[:, :, :], 0.0, None, ALU.is_ge)
            e.tensor_scalar(grown[:, :], short[:, :], 0.0, None, ALU.is_gt).then_inc(step_done, 1)

        def find_jumps(eng, e, p):
            after_step(eng, p, 3)
            e.tensor_tensor(added[1][:, 4:], added[0][:, 4:], added[0][:, 3:3 + E], ALU.add)
            e.tensor_tensor(filled[:, :], filled[:, :], added[0][:, 4:], ALU.add).then_inc(step_done, 1)
            after_step(eng, p, 4)
            e.tensor_tensor(added[2][:, 4:], added[1][:, 4:], added[1][:, 2:2 + E], ALU.add)
            e.tensor_tensor(origin[:, :], filled[:, :], current[:, :], ALU.add).then_inc(step_done, 1)
            after_step(eng, p, 5)
            e.tensor_tensor(added[3][:, 4:], added[2][:, 4:], added[2][:, 0:E], ALU.add)
            e.tensor_scalar(origin[:, :], origin[:, :], handed_out[:, 0:1], None, ALU.subtract
                            ).then_inc(step_done, 1)
            after_step(eng, p, 6)
            e.tensor_tensor(jump[:, :], added[3][:, 4:], origin[:, :], ALU.subtract)
            e.tensor_tensor(handed_out[:, :], handed_out[:, :], added[3][:, 3 + E:4 + E], ALU.add
                            ).then_inc(step_done, 1)
            after_step(eng, p, 7)

        def find_places(eng, e, p):
            over_pair = lambda a: a[:, :].unsqueeze(1).to_broadcast([128, 2, E])
            e.tensor_tensor(in_new[:, :, :], in_new[:, :, :], over_pair(jump), ALU.mult)
            e.tensor_tensor(grown[:, :], grown[:, :], jump[:, :], ALU.mult)
            eng.drain()
            e.tensor_tensor(place[:, :, :], place[:, :, :], in_new[:, :, :], ALU.add)
            e.tensor_tensor(current[:, :], current[:, :], grown[:, :], ALU.add)
            eng.drain()
            e.tensor_tensor(place[:, :, :], place[:, :, :], onehot[:, :, :], ALU.mult).then_inc(onehot_read, 1)
            for n in (4, 2, 1):
                eng.drain()
                if n == 1 and e is nc.gpsimd:
                    eng.wait_ge(meta_ok, p - 1)
                    eng.wait_ge(row_ok, 2 * (p - 1))
                e.tensor_tensor(place[:, :, 0:n], place[:, :, 0:n], place[:, :, n:2 * n], ALU.add)

        block = stack.enter_context(nc.Block())

        @block.sync
        def _(sp):
            sp.dma_start(x_all[:, 0:FIRST, :], x[0:FIRST, :, :].rearrange("b t d -> t b d")).then_inc(in_x_first, 16)
            sp.dma_start(x_all[:, FIRST:B, :], x[FIRST:B, :, :].rearrange("b t d -> t b d")).then_inc(in_x_rest, 16)

            def write_parts(pair, u, half, out_sem):
                sp.wait_ge(parts_ok, 2 * pair + 2)
                dst = qk_dram[bass.ds(pair, 1), :, :, :, :, :].rearrange(
                    "o q (r d) p i t -> (d p i) (o q r) t", r=SLOTS)
                sp.dma_start(dst, parts(u, half)).then_inc(out_sem, 16)

            def load_qk(pair, c):
                for h in range(2):
                    src = qk_dram[bass.ds(pair, 1), :, :, h, :, :].rearrange("o q k i t -> k (o q) (i t)")
                    dst = qk[c][64 * h:64 * h + ROWS, :, :, :].rearrange("k q i t -> k q (i t)")
                    sp.dma_start(dst, src).then_inc(qk_in, 16)

            def load_expert(e):
                sp.dma_start(w1_sb[:, bass.ds(e * (2 * F), 2 * F)],
                             w1[bass.ds(e, 1), :, :].rearrange("o p f -> (o p) f")).then_inc(in_ffn, 16)
                sp.dma_start(w2_sb[:, bass.ds(e * F, F)].rearrange("p (c d) -> p c d", d=D),
                             w2[bass.ds(e, 1), :, :].rearrange("o (c p) d -> p (o c) d", p=128)
                             ).then_inc(in_ffn, 16)
                sp.dma_start(b1_sb[:, bass.ds(e * (2 * F), 2 * F)],
                             b1[bass.ds(e, 1), :].rearrange("o f -> (o f)").partition_broadcast(128)
                             ).then_inc(in_ffn, 16)

            sp.wait_ge(consts, 1)
            sp.wait_ge(in_ctx, 16)
            sp.dma_start(tiles_dram.rearrange("(j s) w -> s j w", s=S),
                         empty[:, :].unsqueeze(1).to_broadcast([S, TILES, WIDTH])).then_inc(tiles_empty, 16)
            for u in range(2):
                write_parts(u, u, 0, first_out)
            sp.wait_ge(first_out, 32)
            load_qk(0, 0)
            with sp.Fori(1, PAIRS // 2 - 1) as i:
                for u in range(2):
                    write_parts(2 * i + u, u, i, qk_out)
            write_parts(PAIRS - 2, 0, PAIRS // 2 - 1, qk_out)
            sp.wait_ge(qk_in, 32)
            load_qk(1, 1)
            write_parts(PAIRS - 1, 1, PAIRS // 2 - 1, qk_out)
            sp.wait_ge(qk_out, 16 * (PAIRS - 2))
            def slot_fn(b, p, u, c, now, nxt, prev, prev2, route):
                if now and u == 0 and not (isinstance(p, int) and p in (0, PAIRS - 1)):
                    sp.wait_ge(qk_in, 32 * (p + 1))
                    wait(sp, b_mm, 4 * b)
                    load_qk(p + 1, 1 - c)
                if now and u == 1:
                    load_expert(p)
                if isinstance(b, int) and b == B - 1:
                    sp.dma_start(b2_sb[:, :], b2.partition_broadcast(128)).then_inc(in_ffn, 16)
            run_slots(sp, slot_fn)

            def load_tile(j, q):
                sp.dma_start(got[q][:, :], tiles_dram[bass.ds(j * S, S), :]).then_inc(loaded[q], 16)

            for k in range(2):
                sp.wait_ge(placed[k], 16 * PAIRS)
            for q in range(3):
                load_tile(q, q)

            def step_fn(j, i, q, has):
                if has(3):
                    wait(sp, gotT_mm, j)
                    wait(sp, base_ok, j)
                    load_tile(j + 3, (q + 3) % 4)
            run_tiles(sp, step_fn)

        @block.gpsimd
        def _(pool):
            g = nc.gpsimd
            g.memset(ident[:, :], 0.0)
            g.memset(power[:, :], -0.5)
            g.memset(empty[:, :], 0.0)
            pool.drain()
            g.affine_select(out=ident[:, :], in_=ident[:, :], compare_op=ALU.not_equal, fill=1.0,
                            base=0, pattern=[[-1, 128]], channel_multiplier=1)
            g.memset(ones[:, :], 1.0)
            pool.drain()
            g.memset(empty[:, TOKEN_COL:TOKEN_COL + 1].bitcast(u32), NO_TOKEN).then_inc(consts, 1)

            def rstd_of_x(k, lo, hi):
                pool.wait_ge(x_var, k + 1)
                g.tensor_scalar(var1[:, lo:hi], mv1[:, lo:hi, 1], EPS, None, ALU.add)
                pool.drain()
                g.tensor_tensor(rstd1[:, lo:hi], var1[:, lo:hi], power[:, lo:hi], ALU.pow).then_inc(x_rstd, 1)

            rstd_of_x(0, 0, FIRST)
            g.memset(ones_bf[:, :], 1.0)
            g.memset(pick[:, :], 0.0)
            g.memset(eps[:, :], EPS)
            g.memset(seen[:, :], 0.0)
            for t in (filled, current, handed_out, *added):
                g.memset(t[:, :], 0.0)
            g.memset(zero[:, :], 0)
            for u in range(2):
                g.memset(maxparts[u][:, :, :, :], 0.0)
                g.memset(vpad[u][:, :, :], 0.0)
            pool.drain()
            g.affine_select(out=below[:, :], in_=ones_bf[:, :], compare_op=ALU.is_gt, fill=0.0,
                            base=0, pattern=[[1, 128]], channel_multiplier=-1)
            g.iota(number[:, :], pattern=[[1, E]], base=0, channel_multiplier=0,
                   allow_small_or_imprecise_dtypes=True)
            g.iota(token_no[:, :], pattern=[[S, 2]], base=0, channel_multiplier=1)
            for u in range(2):
                g.memset(vpad[u][:, :, HD:HD + 1], 1.0)
            rstd_of_x(1, FIRST, B)
            for h in range(2):
                for a in range(PARTS):
                    half = pick[:, HALF * h:HALF * (h + 1)]
                    g.affine_select(out=half, in_=half, compare_op=ALU.not_equal,
                                    fill=-1.0, base=-(64 * h + HALF * a),
                                    pattern=[[-1, HALF]], channel_multiplier=1)
                    pool.drain()
            g.tensor_copy(ident_bf[:, :], ident[:, :]).then_inc(consts, 1)

            with pool.Fori(0, PAIRS // 2) as i:
                for u in range(2):
                    pair = 2 * i + u
                    pool.wait_ge(high_ok, pair + 1)
                    g.tensor_tensor(resid[u][:, :, :], qkf[u][:, :, :], high[u][:, :, :],
                                    ALU.subtract).then_inc(resid_ok, 1)

            pool.wait_ge(obias_ready, 1)

            def scatter_rows(q, c):
                pool.drain()
                g.tensor_copy(place_at[:, :].unsqueeze(2), place[:, :, 0:1]).then_inc(places_found, 1)
                pool.drain()
                for k in range(2):
                    g.indirect_dma_start(tiles_dram[:, :], bass.IndirectOffsetOnAxis(place_at[:, k:k + 1], 0),
                                         rows[:, 2 * c + k, :], None).then_inc(placed[k], 16)

            def slot_fn(b, p, u, c, now, nxt, prev, prev2, route):
                if now:
                    xb = xb_all[:, bass.ds(b, 1), :].rearrange("t o d -> t (o d)")
                    g.tensor_tensor(xb, xb, obias[:, :], ALU.add).then_inc(xb_ready, 1)
                if prev2:
                    pool.wait_ge(x2_var, b - 1)
                    g.tensor_tensor(var2[u][:, :], mv2[u][:, 1:2], eps[:, :], ALU.add).then_inc(eps_added, 1)
                    pool.wait_ge(eps_added, b - 1)
                    g.tensor_tensor(rstd2[u][:, :], var2[u][:, :], power[:, 0:1], ALU.pow).then_inc(x2_rstd, 1)
                if route and not (isinstance(p, int) and p == PAIRS + 1):
                    hand_out(pool, g, p)
                if u == 1 and before(b, 5):
                    find_jumps(pool, g, p)
                    find_places(pool, g, p)
                    scatter_rows(p - 2, c)
            pool.wait_ge(tiles_empty, 16)
            run_slots(pool, slot_fn)
            pool.wait_ge(places_found, PAIRS)
            pool.wait_ge(meta_ok, PAIRS)
            pool.wait_ge(row_ok, B)
            for k in range(2):
                g.indirect_dma_start(tiles_dram[:, :], bass.IndirectOffsetOnAxis(last_places[:, k:k + 1], 0),
                                     rows[:, 2 * ((PAIRS - 1) % 2) + k, :], None).then_inc(placed[k], 16)
            pool.wait_ge(in_ffn, 16 * N_IN_FFN)

            def note_expert(j, i, q, used):
                pool.wait_ge(loaded[q], 16 * (i + 1))
                wait(pool, y_mm, used)
                g.tensor_tensor(expert[q][:, :], got[q][0:1, EXPERT_COL:WIDTH].bitcast(u32), zero[0:1, 0:1],
                                ALU.add).then_inc(expert_ok, 1)

            note_expert(0, 0, 0, 0)

            def step_fn(j, i, q, has):
                if has(1):
                    note_expert(j + 1, i + (q + 1) // 4, (q + 1) % 4, j - 2)
                if has(0):
                    wait(pool, scattered[q], 16 * i)
                    pool.wait_ge(expert_ok, j + 1)
                    g.tensor_tensor(numbers[q][:, :], got[q][:, TOKEN_COL:EXPERT_COL].bitcast(u32), zero[:, 0:1],
                                    ALU.add)
                    e = pool.value_load(got[q][0:1, EXPERT_COL:WIDTH].bitcast(i32), min_val=0, max_val=E - 1)
                    wait(pool, base_ok, j - 1)
                    wait(pool, final_ok, j - 1)
                    g.tensor_tensor(base[q][:, :], got[q][:, 0:D], b2_sb[:, bass.ds(e * D, D)],
                                    ALU.add).then_inc(base_ok, 1)
                elif has(-2):
                    pool.wait_ge(final_ok, j - 1)
                if has(-2):
                    k = (q - 2) % 4
                    g.indirect_dma_start(out, bass.IndirectOffsetOnAxis(numbers[k][:, :], 0),
                                         final[k][:, :], None, bounds_check=TOKENS - 1,
                                         oob_is_err=False).then_inc(scattered[k], 16)
            run_tiles(pool, step_fn)
            for q in range(4):
                pool.wait_ge(scattered[q], 16 * ((TILES - q + 3) // 4))

        @block.scalar
        def _(act):
            a = nc.scalar
            act.dma_start(columns_sb[:, :], columns).then_inc(in_w, 16)
            act.dma_start(row_vectors_sb[:, :], row_vectors.partition_broadcast(128)).then_inc(in_w, 16)
            act.dma_start(ctx_all[:, :, :], ctx_in.rearrange("b t d -> t b d")).then_inc(in_ctx, 16)
            act.wait_ge(in_x_first, 16)
            a.copy(var2[0][:, :], x_all[:, 0, 0:1])
            act.wait_ge(in_w, 32)

            def evac_T(pair, u):
                act.wait_ge(T_mm, pair + 1)
                wait(act, V_mm, pair - 1)
                a.copy(stagedT[u][:, :], bank[u][:, :]).then_inc(T_ok, 1)

            def evac_P(pair, u, half):
                act.wait_ge(P_mm, pair + 1)
                wait(act, resid_ok, pair - 1)
                a.activation(qkf[u][:, 0, :], bank[2 + u][:, 0:2 * S], ACT.Identity, bias=bq_sb[:, 0:1])
                a.activation(qkf[u][:, 1, :], bank[2 + u][:, 2 * S:4 * S], ACT.Identity,
                             bias=bk_sb[:, 0:1]).then_inc(qkf_ok, 1)
                act.wait_ge(qkf_ok, pair + 1)
                wait(act, parts_ok, 2 * pair - 2)
                a.copy(high[u][:, :, :], qkf[u][:, :, :]).then_inc(high_ok, 1)
                act.wait_ge(V_mm, pair + 1)
                a.copy(v_all[:, bass.ds(2 * pair, 2), :].rearrange("k b d -> k (b d)"),
                       bank[4 + u][:, 0:2 * D]).then_inc(v_ok, 1)

            def slot_fn(b, p, u, c, now, nxt, prev, prev2, route):
                def exps(f):
                    act.wait_ge(b_mm, 4 * b + f + 1)
                    wait(act, pv_mm, 4 * b + f - 3)
                    a.activation(probsT[f][:, :], bank[2 + f % 2][:, :], ACT.Exp,
                                 scale=float(HD) ** -0.5).then_inc(probs_ok, 1)
                for f in range(4):
                    if now:
                        exps(f)
                    if nxt and f == 1:
                        wait(act, pv_mm, 4 * b)
                        a.copy(vpad[1 - u][:, :, 0:HD], v_all[:, bass.ds(b + 1, 1), :].rearrange(
                            "k o (h c) -> k (o h) c", h=HEADS)).then_inc(vpad_ok, 1)
                if prev2:
                    act.wait_ge(x2T_mm, b - 1)
                    wait(act, lg_mm, b - 2)
                    a.copy(x2T[:, :], bank[7][:, 0:S]).then_inc(x2T_ok, 1)
                if prev:
                    act.wait_ge(attT_mm, b)
                    wait(act, wo_mm, b - 1)
                    a.copy(attT[:, :], bank[6][:, 0:S]).then_inc(attT_ok, 1)
                if nxt:
                    act.wait_ge(maxT_mm, b + 2)
                    a.copy(maxT[1 - u][:, :], bank[7][:, 0:S // 2].bitcast(bf16)).then_inc(maxT_ok, 1)
                if now:
                    act.wait_ge(pv_mm, 4 * b + 4)
                    wait(act, o_mm, b)
                    a.copy(oT[:, :], bank[4][:, :]).then_inc(oT_ok, 1)
                if prev2:
                    act.wait_ge(x2n_ok, b - 1)
                    if before(b, 6):
                        act.wait_ge(placed[u], 16 * (p - 2))
                    a.copy(rows[:, 2 * (1 - c) + u, 0:2 * D], x2[u][:, :]).then_inc(row_ok, 1)
            run_front(act, evac_T, evac_P)
            act.wait_ge(v_ok, PAIRS)
            act.wait_ge(consts, 2)
            slot(slot_fn, -1)
            run_slots(act, slot_fn)

            def step_fn(j, i, q, has):
                u = q % 2
                if has(1):
                    act.wait_ge(gotT_mm, j + 2)
                    wait(act, h_mm, j)
                    a.copy(gotT[1 - u][:, :], bank[6][:, 0:S]).then_inc(gotT_ok, 1)
                if has(0):
                    act.wait_ge(gate_ok, j + 1)
                    wait(act, hid_ok, j - 1)
                    a.activation(sig[u][:, :], gate[u][:, :], ACT.Sigmoid).then_inc(sig_ok, 1)
                if has(-1):
                    act.wait_ge(hidT_mm, j)
                    wait(act, y_mm, j - 2)
                    a.copy(hidT[1 - u][:, :], bank[5 - u][:, :]).then_inc(hidT_ok, 1)
            a.activation(mv2[0][:, 0:1], mv2[0][:, 1:2], ACT.Sigmoid)
            act.wait_ge(gotT_mm, 1)
            a.copy(gotT[0][:, :], bank[6][:, 0:S]).then_inc(gotT_ok, 1)
            run_tiles(act, step_fn)

        @block.vector
        def _(dve):
            v = nc.vector
            for c in range(2):
                v.memset(qk[c][:, :, :, :], 0.0)
            for landed, batches in ((in_x_first, range(FIRST)), (in_x_rest, range(FIRST, B))):
                dve.wait_ge(landed, 16)
                for b in batches:
                    v.bn_stats(stats1[:, b, :], x_all[:, b, :])
                dve.drain()
                for b in batches:
                    last = v.bn_aggr(mv1[:, b, :], stats1[:, b, :])
                last.then_inc(x_var, 1)
            dve.wait_ge(consts, 1)
            dve.wait_ge(in_w, 32)
            v.tensor_scalar(bv_cols[:, :], ones[:, :], bv_sb[:, 0:1], None, ALU.mult).then_inc(bv_ready, 1)
            dve.wait_ge(in_ctx, 16)
            dve.wait_ge(x_rstd, 1)

            def stage(pair, u):
                wait(dve, T_mm, pair - 1)
                if isinstance(pair, int) and 2 * pair == FIRST:
                    dve.wait_ge(x_rstd, 2)
                for k in range(2):
                    b = bass.ds(2 * pair + k, 1)
                    v.tensor_scalar(staged[u][:, k, :], x_all[:, b, :].rearrange("t o d -> t (o d)"),
                                    mv1[:, b, 0:1].rearrange("t o d -> t (o d)"), rstd1[:, b],
                                    ALU.subtract, ALU.mult)
                v.tensor_copy(staged[u][:, 2:4, :], ctx_all[:, bass.ds(2 * pair, 2), :]).then_inc(staged_ok, 1)

            def split(pair, u, half):
                s = parts(u, half)
                dve.wait_ge(high_ok, pair + 1)
                v.tensor_copy(s[:, 1:6:2, :], high[u][:, 0:1, :].to_broadcast([128, 3, 2 * S]))
                v.tensor_copy(s[:, 6:9, :], high[u][:, 1:2, :].to_broadcast([128, 3, 2 * S]))
                dve.wait_ge(resid_ok, pair + 1)
                v.tensor_copy(s[:, 0:10:9, :], resid[u][:, :, :])
                dve.drain()
                v.tensor_tensor(s[:, 2:12:9, :], resid[u][:, :, :], s[:, 0:10:9, :], ALU.subtract
                                ).then_inc(parts_ok, 1)
                v.tensor_copy(s[:, 4:11:6, :], s[:, 0:10:9, :]).then_inc(parts_ok, 1)

            def slot_fn(b, p, u, c, now, nxt, prev, prev2, route):
                w = 1 - u

                def maxes(f):
                    dve.wait_ge(a_mm, 4 * b + f + 5)
                    v.tensor_reduce(rowmax[w][:, 4 * f:4 * f + 4],
                                    bank[f % 2][:, :].rearrange("t (j k) -> t j k", j=4), X, ALU.max
                                    ).then_inc(max_ok, 1)
                if nxt:
                    maxes(0)
                if route:
                    dve.wait_ge(lg_read, b - 2)
                if prev2:
                    dve.wait_ge(wo_read, b - 1)
                    v.bn_stats(stats2[:, :], x2[u][:, 0:D])
                if route:
                    for k in range(2):
                        v.max(top[:, k, :], logits[:, k, :])
                if prev2 or route:
                    dve.drain()
                if prev2:
                    v.bn_aggr(mv2[u][:, :], stats2[:, :]).then_inc(x2_var, 1)
                if route:
                    for k in range(2):
                        v.max_index(topi[:, k, :], top[:, k, :], logits[:, k, :])
                    dve.drain()
                    wait(dve, onehot_read, p - 2)
                    v.tensor_tensor(onehot[:, :, :], number[:, :].unsqueeze(1).to_broadcast([128, 2, E]),
                                    topi[:, :, 0:1].to_broadcast([128, 2, E]), ALU.is_equal
                                    ).then_inc(onehot_ok, 1)
                if nxt:
                    maxes(1)
                if prev:
                    dve.wait_ge(o_mm, b)
                    o = bank[5][:, :].rearrange("t (h c) -> t h c", c=32)
                    v.reciprocal(rsum[:, :], o[:, :, HD])
                    dve.drain()
                    wait(dve, attT_mm, b - 1)
                    v.tensor_tensor(att[:, :, :], o[:, :, 0:HD],
                                    rsum[:, :].unsqueeze(2).to_broadcast([128, HEADS, HD]),
                                    ALU.mult).then_inc(att_ok, 1)
                if nxt:
                    maxes(2)
                if prev2:
                    dve.wait_ge(x2_rstd, b - 1)
                    v.tensor_scalar(x2[u][:, D:2 * D], x2[u][:, 0:D], mv2[u][:, 0:1], rstd2[u][:, 0:1],
                                    ALU.subtract, ALU.mult).then_inc(x2n_ok, 1)
                if route:
                    dve.wait_ge(rank_mm, p - 1)
                    v.tensor_copy(counts[:, :], bank[6][:, 0:3 * E]).then_inc(rank_read, 1)
                if nxt:
                    maxes(3)
                mp = maxparts[w]
                top_in = rowmax[w][:, :].rearrange("t (p i) -> t p i", p=2)
                res = maxres[w][:, :].rearrange("t (p i) -> t p i", p=2)
                meta = rows[:, 2 * c:2 * c + 2, :]
                dve.drain()
                if nxt:
                    v.tensor_copy(mp[:, :, 0, :], top_in)
                    dve.drain()
                    v.tensor_tensor(res, top_in, mp[:, :, 0, :], ALU.subtract)
                    dve.drain()
                    v.tensor_copy(mp[:, :, 1, :], res)
                    dve.drain()
                    v.tensor_tensor(mp[:, :, 2, :], res, mp[:, :, 1, :], ALU.subtract).then_inc(maxparts_ok, 1)
                if route and before(b, 8):
                    for k in range(2):
                        dve.wait_ge(placed[k], 16 * (p - 3))
                if route:
                    v.tensor_tensor(seen[:, :], seen[:, :], onehot[:, 0, :], ALU.add)
                    v.tensor_copy(meta[:, :, TOKEN_COL:EXPERT_COL].bitcast(u32), token_no[:, :].unsqueeze(2))
                    v.tensor_copy(meta[:, :, EXPERT_COL:WIDTH].bitcast(u32), topi[:, :, 0:1]).then_inc(meta_ok, 1)
                    dve.drain()
                    v.tensor_tensor(seen[:, :], seen[:, :], onehot[:, 1, :], ALU.add)
                    v.tensor_scalar(token_no[:, :], token_no[:, :], 2 * S, None, ALU.add)
                if prev:
                    wait(dve, row_ok, b - 2)
                    dve.wait_ge(wo_mm, b)
                    dve.wait_ge(xb_ready, b)
                    v.tensor_tensor(x2[w][:, 0:D], bank[6][:, 0:D],
                                    xb_all[:, bass.ds(b - 1, 1), :].rearrange("t o d -> t (o d)"), ALU.add
                                    ).then_inc(wo_read, 1)
                if prev2:
                    dve.wait_ge(lg_mm, b - 1)
                    v.tensor_tensor(logits[:, u, :], bank[5][:, 0:E], rb_sb[:, :], ALU.add).then_inc(lg_read, 1)

            def first_maxima():
                dve.wait_ge(obias_mm, 1)
                v.tensor_tensor(obias[:, :], bank[6][:, 0:D], bo_sb[:, :], ALU.add).then_inc(obias_ready, 1)
                slot(slot_fn, -1)
            run_front(dve, stage, split, depth=3, before_last=first_maxima)
            run_slots(dve, slot_fn)
            dve.wait_ge(places_found, PAIRS - 1)
            hand_out(dve, v, PAIRS + 1)
            find_jumps(dve, v, PAIRS + 1)
            find_places(dve, v, PAIRS + 1)
            dve.drain()
            v.tensor_copy(last_places[:, :].unsqueeze(2), place[:, :, 0:1]).then_inc(places_found, 1)
            dve.wait_ge(in_ffn, 16 * N_IN_FFN)
            dve.wait_ge(expert_ok, 1)

            def step_fn(j, i, q, has):
                u = q % 2
                if has(0):
                    e = dve.value_load(expert[q][0:1, 0:1].bitcast(i32), min_val=0, max_val=E - 1)
                    dve.wait_ge(h_mm, j + 1)
                    v.tensor_tensor(gate[u][:, :], bank[1 + 2 * u][:, :],
                                    b1_sb[:, bass.ds(e * (2 * F) + F, F)], ALU.add).then_inc(gate_ok, 1)
                    v.tensor_tensor(up[u][:, :], bank[2 * u][:, :],
                                    b1_sb[:, bass.ds(e * (2 * F), F)], ALU.add).then_inc(up_ok, 1)
                if has(-2):
                    k = (q - 2) % 4
                    dve.wait_ge(y_mm, j - 1)
                    dve.wait_ge(base_ok, j - 1)
                    v.tensor_tensor(final[k][:, :], bank[7][:, 0:D], base[k][:, :], ALU.add).then_inc(final_ok, 1)
                if has(0):
                    if has(1):
                        dve.wait_ge(expert_ok, j + 2)
                    dve.wait_ge(sig_ok, j + 1)
                    dve.wait_ge(up_ok, j + 1)
                    wait(dve, hidT_mm, j - 1)
                    v.tensor_tensor(hid[u][:, :], up[u][:, :], sig[u][:, :], ALU.mult).then_inc(hid_ok, 1)
            run_tiles(dve, step_fn)

        @block.tensor
        def _(pe):
            t = nc.tensor
            pe.wait_ge(consts, 1)
            pe.wait_ge(in_w, 32)

            def transposes(pair, u):
                pe.wait_ge(staged_ok, pair + 1)
                wait(pe, T_ok, pair - 1)
                for k in range(4):
                    last = t.transpose(bank[u][:, k * S:(k + 1) * S], staged[u][:, k, :], ident[:, :])
                last.then_inc(T_mm, 1)

            def project(pair, u, half):
                pe.wait_ge(T_ok, pair + 1)
                wait(pe, qkf_ok, pair - 1)
                t.matmul(bank[2 + u][:, 0:2 * S], wq_sb[:, :], stagedT[u][:, 0:2 * S], start=True, stop=True)
                t.matmul(bank[2 + u][:, 2 * S:4 * S], wk_sb[:, :], stagedT[u][:, 2 * S:4 * S],
                         start=True, stop=True).then_inc(P_mm, 1)
                wait(pe, v_ok, pair - 1)
                for k in range(2):
                    last = t.matmul(bank[4 + u][:, k * D:(k + 1) * D], stagedT[u][:, (2 + k) * S:(3 + k) * S],
                                    wv_sb[:, :], start=True, stop=True)
                last.then_inc(V_mm, 1)

            def slot_fn(b, p, u, c, now, nxt, prev, prev2, route):
                w = 1 - u
                this_qk = qk[c][:, :, :, u * S:(u + 1) * S]
                next_qk = qk[c if u == 0 else 1 - c][:, :, :, w * S:(w + 1) * S]

                def scores_for_max(f):
                    if f == 0 and u == 1:
                        pe.wait_ge(qk_in, 32 * (p + 2))
                    wait(pe, max_ok, 4 * b + f + 3)
                    lo = 64 * (f // 2)
                    for j in range(4):
                        i = 4 * (f % 2) + j
                        last = t.matmul(bank[f % 2][:, j * S:(j + 1) * S], next_qk[lo:lo + DEPTH, 0, i, :],
                                        next_qk[lo:lo + DEPTH, 1, i, :], start=True, stop=True)
                    last.then_inc(a_mm, 1)

                def scores_T(f):
                    wait(pe, probs_ok, 4 * b + f - 1)
                    if f == 0:
                        pe.wait_ge(maxT_ok, b + 1)
                    lo = 64 * (f // 2)
                    for j in range(4):
                        i = 4 * (f % 2) + j
                        dst = bank[2 + f % 2][:, j * S:(j + 1) * S]
                        t.matmul(dst, this_qk[lo:lo + DEPTH, 1, i, :], this_qk[lo:lo + DEPTH, 0, i, :],
                                 start=True, stop=False)
                        last = t.matmul(dst, pick[:, 4 * f + j:4 * f + j + 1].to_broadcast([128, S]), maxT[u][:, :],
                                        start=False, stop=True)
                    last.then_inc(b_mm, 1)

                def times_v(f):
                    pe.wait_ge(probs_ok, 4 * b + f + 1)
                    if f == 0:
                        pe.wait_ge(vpad_ok, b + 1)
                    for j in range(4):
                        last = t.matmul(bank[4][32 * j:32 * j + 32, f * S:(f + 1) * S], vpad[u][:, 4 * f + j, :],
                                        probsT[f][:, j * S:(j + 1) * S], start=True, stop=True)
                    last.then_inc(pv_mm, 1)

                def back_to_queries():
                    pe.wait_ge(oT_ok, b)
                    wait(pe, lg_read, b - 2)
                    for f in range(4):
                        last = t.transpose(bank[5][:, f * S:(f + 1) * S], oT[:, f * S:(f + 1) * S], ident[:, :])
                    last.then_inc(o_mm, 1)

                def ranks():
                    pe.wait_ge(onehot_ok, p - 1)
                    if prev:
                        pe.wait_ge(wo_read, b - 1)
                    r = bank[6]
                    t.matmul(r[:, 0:E], below[:, :], onehot[:, 0, :], start=True, stop=False)
                    t.matmul(r[:, 0:E], ones_bf[:, :], seen[:, :], start=False, stop=True)
                    t.matmul(r[:, E:2 * E], below[:, :], onehot[:, 1, :], start=True, stop=False)
                    t.matmul(r[:, E:2 * E], ones_bf[:, :], onehot[:, 0, :], start=False, stop=False)
                    t.matmul(r[:, E:2 * E], ones_bf[:, :], seen[:, :], start=False, stop=True)
                    for k in range(2):
                        t.matmul(r[:, 2 * E:3 * E], ones_bf[:, :], onehot[:, k, :], start=(k == 0), stop=False)
                    t.matmul(r[:, 2 * E:3 * E], ones_bf[:, :], seen[:, :], start=False, stop=True
                             ).then_inc(rank_mm, 1)

                if nxt:
                    scores_for_max(0)
                if now:
                    scores_T(0)
                if nxt:
                    scores_for_max(1)
                if now:
                    scores_T(1)
                if prev:
                    back_to_queries()
                if nxt:
                    scores_for_max(2)
                if now:
                    scores_T(2)
                if nxt:
                    scores_for_max(3)
                if now:
                    times_v(0)
                if route:
                    ranks()
                if now:
                    scores_T(3)
                    times_v(1)
                if prev2:
                    pe.wait_ge(x2n_ok, b - 1)
                    t.transpose(bank[7][:, 0:S], x2[u][:, D:2 * D], ident[:, :]).then_inc(x2T_mm, 1)
                if now:
                    times_v(2)
                if prev:
                    pe.wait_ge(att_ok, b)
                    wait(pe, wo_read, b - 1)
                    if route:
                        pe.wait_ge(rank_read, p - 1)
                    t.transpose(bank[6][:, 0:S], att[:, :, :].rearrange("t h c -> t (h c)"),
                                ident[:, :]).then_inc(attT_mm, 1)
                if prev2:
                    pe.wait_ge(x2T_ok, b - 1)
                    if not prev:
                        pe.wait_ge(lg_read, b - 2)
                    t.matmul(bank[5][:, 0:E], x2T[:, :], rw_sb[:, :], start=True, stop=True).then_inc(lg_mm, 1)
                if prev:
                    pe.wait_ge(attT_ok, b)
                    t.matmul(bank[6][:, 0:D], attT[:, :], wo_sb[:, :], start=True, stop=True).then_inc(wo_mm, 1)
                if nxt:
                    pe.wait_ge(maxparts_ok, b + 2)
                    t.transpose(bank[7][:, 0:S // 2].bitcast(bf16), maxparts[w][:, :, :, :].rearrange(
                        "t p a i -> t (p a i)"), ident_bf[:, :]).then_inc(maxT_mm, 1)
                if now:
                    times_v(3)

            run_front(pe, transposes, project)
            pe.wait_ge(bv_ready, 1)
            t.matmul(bank[6][:, 0:D], bv_cols[:, :], wo_sb[:, :], start=True, stop=True).then_inc(obias_mm, 1)
            pe.wait_ge(T_ok, PAIRS)
            pe.wait_ge(consts, 2)
            slot(slot_fn, -1)
            pe.wait_ge(qkf_ok, PAIRS)
            pe.wait_ge(v_ok, PAIRS)
            pe.wait_ge(obias_ready, 1)
            run_slots(pe, slot_fn)

            pe.wait_ge(in_ffn, 16 * N_IN_FFN)

            def tile_T(j, q, i):
                pe.wait_ge(loaded[q], 16 * (i + 1))
                t.transpose(bank[6][:, 0:S], got[q][:, D:2 * D], ident[:, :]).then_inc(gotT_mm, 1)

            tile_T(0, 0, 0)
            pe.wait_ge(expert_ok, 1)

            def step_fn(j, i, q, has):
                u = q % 2
                if has(0):
                    e = pe.value_load(expert[q][0:1, 0:1].bitcast(i32), min_val=0, max_val=E - 1)
                    pe.wait_ge(gotT_ok, j + 1)
                    wait(pe, up_ok, j - 1)
                    for k in range(2):
                        last = t.matmul(bank[2 * u + k][:, :], gotT[u][:, :],
                                        w1_sb[:, bass.ds(e * (2 * F) + k * F, F)], start=True, stop=True)
                    last.then_inc(h_mm, 1)
                if has(1):
                    tile_T(j + 1, (q + 1) % 4, i + (q + 1) // 4)
                if has(-2):
                    e2 = pe.value_load(expert[(q - 2) % 4][0:1, 0:1].bitcast(i32), min_val=0, max_val=E - 1)
                    pe.wait_ge(hidT_ok, j - 1)
                    wait(pe, final_ok, j - 2)
                    for c in range(4):
                        last = t.matmul(bank[7][:, 0:D], hidT[u][:, c * 128:(c + 1) * 128],
                                        w2_sb[:, bass.ds(e2 * F + c * D, D)], start=(c == 0), stop=(c == 3))
                    last.then_inc(y_mm, 1)
                if has(1):
                    pe.wait_ge(expert_ok, j + 2)
                if has(-1):
                    pe.wait_ge(hid_ok, j)
                    for c in range(4):
                        last = t.transpose(bank[5 - u][:, c * 128:(c + 1) * 128],
                                           hid[1 - u][:, c * 128:(c + 1) * 128], ident[:, :])
                    last.then_inc(hidT_mm, 1)
            run_tiles(pe, step_fn)


def kernel(x, ctx_1024, L0_xattn_Wq, L0_xattn_bq, L0_xattn_Wk, L0_xattn_bk, L0_xattn_Wv, L0_xattn_bv,
           L0_xattn_Wo, L0_xattn_bo, L0_ffn_router_w, L0_ffn_router_b, L0_ffn_w1, L0_ffn_b1, L0_ffn_w2,
           L0_ffn_b2):
    import numpy as np
    import concourse.bacc as bacc
    from concourse.bass_utils import run_bass_kernel_spmd

    order = np.arange(D).reshape(HEADS, HD).T.reshape(-1)
    arrays = {
        "x": x, "ctx": ctx_1024,
        "columns": np.concatenate(
            [np.asarray(L0_xattn_Wq)[order].T, np.asarray(L0_xattn_Wk)[order].T, np.asarray(L0_xattn_Wv).T,
             np.asarray(L0_xattn_Wo).T, np.asarray(L0_ffn_router_w), np.asarray(L0_xattn_bq)[order, None],
             np.asarray(L0_xattn_bk)[order, None], np.asarray(L0_xattn_bv)[:, None]], axis=1),
        "row_vectors": np.concatenate([np.asarray(L0_xattn_bo), np.asarray(L0_ffn_router_b)]),
        "w1": L0_ffn_w1, "b1": L0_ffn_b1,
        "w2": L0_ffn_w2, "b2": np.asarray(L0_ffn_b2).reshape(-1),
    }
    arrays = {n: np.ascontiguousarray(a) for n, a in arrays.items()}
    nc = bacc.Bacc("TRN2", target_bir_lowering=False, num_devices=1)
    args = [nc.dram_tensor(n, a.shape, mybir.dt.from_np(a.dtype), kind="ExternalInput").ap()
            for n, a in arrays.items()]
    out = nc.dram_tensor("out", (TOKENS, D), mybir.dt.float32, kind="ExternalOutput").ap()
    xattn_ffn(nc, *args, out)
    r = run_bass_kernel_spmd(nc, [arrays], core_ids=[0])
    return r.results[0]["out"].reshape(B, S, D)
```
